# Optimizing a Trainium2 kernel written in Bass

```python
import numpy as np
import jax
import jax.numpy as jnp

def _softmax(x, axis=-1):
    return jax.nn.softmax(x, axis=axis)
def _gelu(x):
    return jax.nn.gelu(x, approximate=True)
def _silu(x):
    return jax.nn.silu(x)
def _sigmoid(x):
    return jax.nn.sigmoid(x)
def _layernorm(x, axis=-1, eps=1e-5):
    m = jnp.mean(x, axis=axis, keepdims=True)
    v = jnp.var(x, axis=axis, keepdims=True)
    return (x - m) / jnp.sqrt(v + eps)
def _scatter_add(tgt, idx, src, axis=0):
    return tgt.at[idx].add(src)
def _segment_sum(src, seg, n):
    return jax.ops.segment_sum(src, seg, n)

kernel_name = 'mk_adj_preln_d1_adj_256_60d84c'

def setup_inputs(seed: int = 0):
    np.random.seed(seed)
    _w = jnp.asarray
    def _rec_inputs():
        import jax
        import jax.numpy as jnp
        _gk = jax.random.key(seed)
        x = -0.0005207 + 1.001 * jax.random.normal(jax.random.fold_in(_gk, 1), (8192, 256), jnp.float32)
        _a = jax.random.bernoulli(jax.random.fold_in(_gk, 2), 0.00390625, (8192, 8192))
        adj = _a.astype(jnp.int32)
        return x, adj
    x, adj = _rec_inputs()
    def _L0_gnn_setup():
        import jax, jax.numpy as jnp
        import numpy as np
        NEG_INF = -9000000000000000.0
        key = jax.random.key(seed)
        k1, k2, k3, k4 = jax.random.split(key, 4)
        N, F = (8192, 256)
        node = jax.random.normal(k1, (N, F), dtype=jnp.float32)
        adj = jax.random.randint(k2, (N, N), 0, 2, dtype=jnp.int32)
        W = jax.random.normal(k3, (F, F), dtype=jnp.float32) * (1.0 / np.sqrt(F))
        a = jax.random.normal(k4, (2 * F, 1), dtype=jnp.float32) * (1.0 / np.sqrt(F))
        return {'node': node, 'adj': adj, 'W': W, 'a': a}
    _L0_gnn_all = _L0_gnn_setup()
    _L0_gnn_in = {k: v for k, v in _L0_gnn_all.items() if k in ('W', 'a', )}
    del _L0_gnn_all

    return {
        "x": x,
        "adj": adj,
        "L0_gnn_W": _L0_gnn_in["W"],
        "L0_gnn_a": _L0_gnn_in["a"],
    }

def reference(x, adj, L0_gnn_W, L0_gnn_a):
    import jax
    import jax.numpy as jnp
    def _L0_gnn_ref(node, adj, W, a):
        import jax, jax.numpy as jnp
        import numpy as np
        NEG_INF = -9000000000000000.0
        h = node @ W
        Fdim = W.shape[0]
        s1 = h @ a[:Fdim, 0]
        s2 = h @ a[Fdim:, 0]
        e = jax.nn.leaky_relu(s1[:, None] + s2[None, :], negative_slope=0.01)
        e = jnp.where(adj > 0, e, jnp.float32(NEG_INF))
        att = jax.nn.softmax(e, axis=1)
        return h + att @ node

    h = jnp.maximum(_layernorm(x, axis=-1), 0.0)
    x = x + _L0_gnn_ref(h, adj, L0_gnn_W, L0_gnn_a)
    return x


_drawn_inputs = setup_inputs


def setup_inputs(seed=0):
    import zlib

    import numpy as np

    out = dict(_drawn_inputs(seed))
    spreads = {}
    factors = {}
    for name, (base, spread) in spreads.items():
        noise = np.random.default_rng([zlib.crc32(name.encode()), seed]).standard_normal(out[name].shape)
        drawn = base * np.exp(spread * noise) if base else spread * noise
        out[name] = jnp.asarray(drawn.astype(out[name].dtype))
    for name, factor in factors.items():
        out[name] = (out[name] * factor).astype(out[name].dtype)
    return out
```

```python
from contextlib import ExitStack

import concourse.bass as bass
from concourse import mybir

P = 128
EPS = 1e-5
SLOPE = 0.01
TINY = 1e-30
ALU = mybir.AluOpType
ACT = mybir.ActivationFunctionType
AX_X = mybir.AxisListType.X
F32 = mybir.dt.float32
F32R = mybir.dt.float32r
I32 = mybir.dt.int32


def gat_layer(nc: bass.Bass, x: bass.AP, adj_t: bass.AP, w: bass.AP, a: bass.AP, out: bass.AP):
    N, F = x.shape
    T = N // P
    NB, _, _, IB = adj_t.shape
    TB = IB // P
    FD = F + 2
    KF = F // P
    G = 8
    XS = 4
    NI = T // G // XS
    U = 8
    Q = T // U
    HS = 4
    LS = 2
    assert TB == 8 and G * F == 2 * IB and Q >= 3

    x_t = x.rearrange("(t p) f -> p t f", p=P)
    out_t = out.rearrange("(t p) f -> p t f", p=P)
    adj_flat = adj_t.rearrange("b t p i -> p (b t) i")
    r_dram = nc.dram_tensor("r_rows", [T, P], F32, kind="Internal").ap()

    with ExitStack() as ctx:
        def sb(name, shape, dt):
            return ctx.enter_context(nc.sbuf_tensor(name, shape, dt))

        def sem(name):
            return ctx.enter_context(nc.semaphore(name))

        node_hi = sb("node_hi", [P, T, FD], F32R)
        node_lo = sb("node_lo", [P, T, F], F32R)
        ring = sb("ring", [P, U, IB], I32)
        w_buf = sb("w_buf", [P, LS, IB], F32)
        p_hi = sb("p_hi", [P, HS, IB], F32R)
        p_lo = sb("p_lo", [P, LS, IB], F32R)
        r_buf = sb("r_buf", [P, 2 * F + KF * FD], F32)
        acc = sb("acc", [P, TB, FD], F32)
        f1 = sb("f1", [P, T], F32)
        f2 = sb("f2", [P, T], F32)
        neg_f1 = sb("neg_f1", [P, T], F32)
        s_cols = sb("s_cols", [P, T, 2], F32)
        tmp = sb("tmp", [P, 2, T], F32)
        ident = sb("ident", [P, P], F32)
        s2_max = sb("s2_max", [P, 2], F32)
        stats = sb("stats", [P, G, 6], F32)
        nrm = sb("nrm", [P, 9, G], F32)
        denom = sb("denom", [P, 2, TB], F32)
        psum = ctx.enter_context(nc.psum_tensor("psum", [P, 8, 512], F32))

        ring_f = ring[:, :, :].bitcast(F32)
        ones = node_hi[:, :, F:FD]
        r_row = r_buf[:, 0:IB]
        xg = [ring_f[:, 2 * s:2 * s + 2, :].rearrange("p a (k f) -> p (a k) f", f=F) for s in range(XS)]
        node = [w_buf[:, :, :].rearrange("p a (k f) -> p (a k) f", f=F), acc[:, :, 0:F]]
        node_t = [r_buf[:, s * F:(s + 1) * F] for s in range(2)]
        wx = r_buf[:, 2 * F:2 * F + KF * FD].rearrange("p (k n) -> p k n", k=KF)
        a_row = acc[:, 0:2, 0:F]
        products = w_buf[:, 0, :].rearrange("p (n f) -> p n f", f=F)
        r_turned = acc[0:T, 0, 0:P]
        mean_diff, mean_sum, squares, var_eps, std, rs0, newton, rstd, shift = (nrm[:, n, :] for n in range(9))
        s1, s2 = s_cols[:, :, 0], s_cols[:, :, 1]

        x_loaded = [sem(f"x_loaded{s}") for s in range(XS)]
        xh_stored = [sem(f"xh_stored{s}") for s in range(XS)]
        weights_loaded = sem("weights_loaded")
        ident_ready = sem("ident_ready")
        ones_ready = sem("ones_ready")
        wx_ready = sem("wx_ready")
        stats_done = sem("stats_done")
        moments_done = sem("moments_done")
        var_ready = sem("var_ready")
        std_ready = sem("std_ready")
        newton_done = sem("newton_done")
        norm_ready = sem("norm_ready")
        node_ready = sem("node_ready")
        hi_ready = sem("hi_ready")
        lo_ready = sem("lo_ready")
        turned = sem("turned")
        node_t_ready = sem("node_t_ready")
        h_ready = sem("h_ready")
        h_used = sem("h_used")
        s2_max_ready = sem("s2_max_ready")
        c_ready = sem("c_ready")
        arguments_ready = sem("arguments_ready")
        exps_ready = sem("exps_ready")
        factors_ready = sem("factors_ready")
        r_ready = sem("r_ready")
        row_loaded = sem("row_loaded")
        adj_loaded = [sem(f"adj_loaded{u}") for u in range(U // 2)]
        w_ready = sem("w_ready")
        t_ready = sem("t_ready")
        p_hi_ready = sem("p_hi_ready")
        p_lo_ready = sem("p_lo_ready")
        step_done = sem("step_done")
        acc_ready = sem("acc_ready")
        acc_free = sem("acc_free")
        denom_done = sem("denom_done")
        scaled = sem("scaled")
        acc_stored = sem("acc_stored")

        block = ctx.enter_context(nc.Block())

        @block.sync
        def _(sp):
            sp.dma_start(wx[:, :, 0:F], w.rearrange("(k p) n -> p k n", p=P)).then_inc(weights_loaded, 16)
            sp.dma_start(a_row, a.rearrange("(s n) o -> (s n o)", s=2).partition_broadcast(P)
                         .rearrange("p (s n) -> p s n", s=2)).then_inc(weights_loaded, 16)
            for s in range(XS):
                sp.dma_start(xg[s], x_t[:, s * G:(s + 1) * G, :]).then_inc(x_loaded[s], 16)
            with sp.Fori(1, NI) as i:
                for s in range(XS):
                    sp.wait_ge(xh_stored[s], 16 * i)
                    sp.dma_start(xg[s], x_t[:, bass.ts(i * XS + s, G), :]).then_inc(x_loaded[s], 16)
            for u in range(U // 2):
                sp.wait_ge(xh_stored[u], 16 * NI)
                sp.dma_start(ring[:, 2 * u:2 * u + 2, :], adj_flat[:, 2 * u:2 * u + 2, :]).then_inc(adj_loaded[u], 16)
            with sp.Fori(1, NB * Q) as n:
                for u in range(U // 2):
                    sp.wait_ge(p_lo_ready, n * U + (2 * u + 2 - U))
                    sp.dma_start(ring[:, 2 * u:2 * u + 2, :],
                                 adj_flat[:, bass.ts(n * (U // 2) + u, 2), :]).then_inc(adj_loaded[u], 16)

        @block.gpsimd
        def _(pool):
            nc.gpsimd.memset(ident[:, :], 0.0).then_inc(ident_ready, 1)
            pool.wait_ge(ident_ready, 1)
            nc.gpsimd.affine_select(out=ident[:, :], in_=ident[:, :], compare_op=ALU.not_equal, fill=1.0, base=0,
                                    pattern=[[-1, P]], channel_multiplier=1).then_inc(ident_ready, 1)
            nc.gpsimd.memset(ones.bitcast(F32), 1.0).then_inc(ones_ready, 1)
            with pool.Fori(0, NI) as i:
                for s in range(XS):
                    pool.wait_ge(h_used, (i * XS + s + 1) * G)
                    pool.dma_start(out_t[:, bass.ts(i * XS + s, G), :], xg[s]).then_inc(xh_stored[s], 16)
            pool.wait_ge(s2_max_ready, 1)
            nc.gpsimd.partition_all_reduce(s2_max[:, 1:2], s2_max[:, 0:1], P, bass.bass_isa.ReduceOp.max)\
                .then_inc(c_ready, 1)

            def load_row(b):
                pool.dma_start(r_row, r_dram.rearrange("t p -> (t p)")[bass.ts(b, IB)].partition_broadcast(P))\
                    .then_inc(row_loaded, 16)

            def add_out(b):
                pool.wait_ge(scaled, b + 1)
                pool.dma_start(out_t[:, bass.ts(b, TB), :], acc[:, :, 0:F], accum_op=ALU.add).then_inc(acc_stored, 16)

            pool.wait_ge(acc_free, TB)
            pool.dma_start(r_dram, r_turned).then_inc(acc_stored, 16)
            pool.wait_ge(acc_stored, 16)
            for s in range(XS):
                pool.wait_ge(xh_stored[s], 16 * NI)
            load_row(0)
            with pool.Fori(0, NB - 1) as b:
                pool.wait_ge(w_ready, (b + 1) * T)
                load_row(b + 1)
                add_out(b)
            add_out(NB - 1)
            pool.wait_ge(acc_stored, 16 * (NB + 1))

        @block.scalar
        def _(act):
            act.wait_ge(wx_ready, KF * 2)
            with act.Fori(0, NI) as i:
                for s in range(XS):
                    g = i * XS + s
                    act.wait_ge(var_ready, g + 1)
                    nc.scalar.activation(std, var_eps, ACT.Sqrt).then_inc(std_ready, 1)
                    act.wait_ge(norm_ready, g + 1)
                    for k in range(G):
                        nc.scalar.activation(node[s % 2][:, k, :], xg[s][:, k, :], ACT.Relu, bias=shift[:, k:k + 1],
                                             scale=rstd[:, k:k + 1]).then_inc(node_ready, 1)
                    act.wait_ge(node_ready, (g + 1) * G)
                    nc.scalar.activation(node_hi[:, bass.ts(g, G), 0:F], node[s % 2], ACT.Copy).then_inc(hi_ready, 1)
                    for k in range(G):
                        act.wait_ge(turned, g * G + k + 1)
                        nc.scalar.activation(node_t[k % 2], psum[:, k % 2, 0:F], ACT.Copy).then_inc(node_t_ready, 1)
            act.wait_ge(arguments_ready, 2)
            nc.scalar.activation(f1[:, :], tmp[:, 0, :], ACT.Exp).then_inc(exps_ready, 1)
            nc.scalar.activation(f2[:, :], tmp[:, 0, :], ACT.Exp, scale=SLOPE).then_inc(exps_ready, 1)
            nc.scalar.activation(s_cols[:, :, 0], tmp[:, 1, :], ACT.Exp, scale=SLOPE - 1.0).then_inc(exps_ready, 1)
            act.wait_ge(factors_ready, 3)

            def weights(step, jt, k, free=True):
                if free:
                    act.wait_ge(t_ready, step - 1)
                nc.scalar.activation(w_buf[:, k % LS, :], r_row, ACT.Relu, bias=neg_f1[:, bass.ts(jt, 1)],
                                     scale=f2[:, bass.ts(jt, 1)]).then_inc(w_ready, 1)

            def high(step, k, free=True):
                act.wait_ge(t_ready, step + 1)
                if free:
                    act.wait_ge(step_done, step - (HS - 1))
                nc.scalar.activation(p_hi[:, k % HS, :], ring_f[:, k, :], ACT.Relu).then_inc(p_hi_ready, 1)

            def take_out(b):
                for it in range(TB):
                    if it < TB - 1:
                        act.wait_ge(acc_ready, b * (TB - 1) + it + 1)
                    else:
                        act.wait_ge(step_done, (b + 1) * T)
                    if it == 0:
                        act.wait_ge(acc_stored, 16 * (b + 1))
                    nc.scalar.activation(acc[:, it, :], psum[:, it, 0:FD], ACT.Copy).then_inc(acc_free, 1)

            def block_of_rows(b, first):
                act.wait_ge(row_loaded, 16 * (b + 1))
                weights(b * T, 0, 0, not first)
                for k in range(U):
                    weights(b * T + k + 1, k + 1, k + 1, not first or k >= 1)
                    high(b * T + k, k, not first or k >= HS)
                    if k == 1 and not first:
                        take_out(b - 1)
                with act.Fori(1, Q - 1) as q:
                    for k in range(U):
                        weights(b * T + q * U + k + 1, q * U + k + 1, k + 1)
                        high(b * T + q * U + k, k)
                for k in range(U):
                    if k < U - 1:
                        weights(b * T + (T - U) + k + 1, T - U + k + 1, k + 1)
                    high(b * T + (T - U) + k, k)

            block_of_rows(0, True)
            with act.Fori(1, NB) as b:
                block_of_rows(b, False)
            take_out(NB - 1)

        @block.vector
        def _(dve):
            dve.wait_ge(weights_loaded, 32)
            for k in range(KF):
                for s in range(2):
                    nc.vector.tensor_tensor_reduce(out=products[:, 2 * k + s, :], in0=wx[:, k, 0:F], in1=a_row[:, s, :], scale=1.0,
                                                   scalar=0.0, op0=ALU.mult, op1=ALU.add,
                                                   accum_out=wx[:, k, F + s:F + s + 1]).then_inc(wx_ready, 1)
            with dve.Fori(0, NI) as i:
                for s in range(XS):
                    g = i * XS + s
                    dve.wait_ge(x_loaded[s], 16 * (i + 1))
                    for k in range(G):
                        last = nc.vector.bn_stats(stats[:, k, :], xg[s][:, k, :])
                    last.then_inc(stats_done, 1)
                    dve.wait_ge(stats_done, g + 1)
                    nc.vector.tensor_tensor(mean_diff, stats[:, :, 1], stats[:, :, 4], ALU.subtract)
                    nc.vector.tensor_tensor(mean_sum, stats[:, :, 1], stats[:, :, 4], ALU.add)
                    nc.vector.tensor_tensor(squares, stats[:, :, 2], stats[:, :, 5], ALU.add).then_inc(moments_done, 1)
                    dve.wait_ge(moments_done, g * 2 + 1)
                    nc.vector.tensor_scalar(squares, squares, 1.0 / F, EPS, ALU.mult, ALU.add)
                    nc.vector.scalar_tensor_tensor(out=mean_diff, in0=mean_diff, scalar=0.25, in1=mean_diff,
                                                   op0=ALU.mult, op1=ALU.mult).then_inc(moments_done, 1)
                    dve.wait_ge(moments_done, g * 2 + 2)
                    nc.vector.tensor_tensor(var_eps, squares, mean_diff, ALU.add).then_inc(var_ready, 1)
                    dve.wait_ge(std_ready, g + 1)
                    nc.vector.reciprocal(rs0, std).then_inc(newton_done, 1)
                    dve.wait_ge(newton_done, g * 5 + 1)
                    nc.vector.tensor_tensor(newton, rs0, rs0, ALU.mult).then_inc(newton_done, 1)
                    dve.wait_ge(newton_done, g * 5 + 2)
                    nc.vector.tensor_tensor(newton, newton, var_eps, ALU.mult).then_inc(newton_done, 1)
                    dve.wait_ge(newton_done, g * 5 + 3)
                    nc.vector.tensor_scalar(newton, newton, -0.5, 1.5, ALU.mult, ALU.add).then_inc(newton_done, 1)
                    dve.wait_ge(newton_done, g * 5 + 4)
                    nc.vector.tensor_tensor(rstd, rs0, newton, ALU.mult).then_inc(newton_done, 1)
                    dve.wait_ge(newton_done, g * 5 + 5)
                    nc.vector.scalar_tensor_tensor(out=shift, in0=mean_sum, scalar=-0.5, in1=rstd, op0=ALU.mult,
                                                   op1=ALU.mult).then_inc(norm_ready, 1)
                    dve.wait_ge(hi_ready, g + 1)
                    nc.vector.tensor_tensor(node_lo[:, bass.ts(g, G), :], node[s % 2],
                                            node_hi[:, bass.ts(g, G), 0:F].bitcast(F32), ALU.subtract)\
                        .then_inc(lo_ready, 1)
                    for k in range(G):
                        dve.wait_ge(h_ready, g * G + k + 1)
                        nc.vector.tensor_copy(s_cols[:, bass.ts(g * G + k, 1), :].rearrange("p o s -> p (o s)"),
                                              psum[:, 4 + k % 4, F:FD])
                        nc.vector.tensor_tensor(xg[s][:, k, :], psum[:, 4 + k % 4, 0:F], xg[s][:, k, :], ALU.add)\
                            .then_inc(h_used, 1)
            dve.wait_ge(h_used, T)
            nc.vector.tensor_reduce(s2_max[:, 0:1], s2, AX_X, ALU.max).then_inc(s2_max_ready, 1)
            dve.wait_ge(c_ready, 1)
            nc.vector.tensor_scalar(tmp[:, 0, :], s2, s2_max[:, 1:2], None, ALU.subtract).then_inc(arguments_ready, 1)
            nc.vector.tensor_scalar(tmp[:, 1, :], s1, s2_max[:, 1:2], 0.0, ALU.add, ALU.max)\
                .then_inc(arguments_ready, 1)
            dve.wait_ge(exps_ready, 3)
            nc.vector.tensor_scalar(neg_f1[:, :], f1[:, :], -0.5, None, ALU.mult).then_inc(factors_ready, 1)
            nc.vector.tensor_scalar(f2[:, :], f2[:, :], 0.5, None, ALU.mult).then_inc(factors_ready, 1)
            nc.vector.tensor_scalar(f1[:, :], f1[:, :], 0.5, None, ALU.mult).then_inc(factors_ready, 1)
            dve.wait_ge(r_ready, 1)
            nc.vector.tensor_copy(r_turned, psum[0:T, 0, 0:P]).then_inc(acc_free, TB)
            dve.wait_ge(factors_ready, 3)

            def masked(step, jt, k, loaded):
                dve.wait_ge(w_ready, step + 1)
                if k % 2 == 0:
                    dve.wait_ge(adj_loaded[k // 2], loaded)
                nc.vector.scalar_tensor_tensor(out=ring_f[:, k, :], in0=w_buf[:, k % LS, :],
                                               scalar=f1[:, bass.ts(jt, 1)], in1=ring[:, k, :], op0=ALU.add,
                                               op1=ALU.min).then_inc(t_ready, 1)

            def low(step, k, free=True):
                dve.wait_ge(p_hi_ready, step + 1)
                if free:
                    dve.wait_ge(step_done, step - (LS - 1))
                nc.vector.scalar_tensor_tensor(out=p_lo[:, k % LS, :], in0=ring_f[:, k, :], scalar=0.0,
                                               in1=p_hi[:, k % HS, :].bitcast(F32), op0=ALU.max, op1=ALU.subtract)\
                    .then_inc(p_lo_ready, 1)

            def normalise(b):
                dve.wait_ge(acc_free, (b + 2) * TB)
                nc.vector.tensor_scalar(denom[:, 0, :], acc[:, :, F], TINY, None, ALU.max).then_inc(denom_done, 1)
                dve.wait_ge(denom_done, 2 * b + 1)
                nc.vector.reciprocal(denom[:, 1, :], denom[:, 0, :]).then_inc(denom_done, 1)
                dve.wait_ge(denom_done, 2 * b + 2)
                for it in range(TB):
                    last = nc.vector.tensor_scalar(acc[:, it, 0:F], acc[:, it, 0:F], denom[:, 1, it:it + 1], None,
                                                   ALU.mult)
                last.then_inc(scaled, 1)

            def block_of_rows(b, first):
                masked(b * T, 0, 0, 16 * (b * Q + 1))
                for k in range(U):
                    turn = b * Q + (2 if k == U - 1 else 1)
                    masked(b * T + k + 1, k + 1, (k + 1) % U, 16 * turn)
                    low(b * T + k, k, not first or k >= LS)
                    if k == 3 and not first:
                        normalise(b - 1)
                with dve.Fori(1, Q - 1) as q:
                    for k in range(U):
                        turn = b * Q + q + (2 if k == U - 1 else 1)
                        masked(b * T + q * U + k + 1, q * U + k + 1, (k + 1) % U, 16 * turn)
                        low(b * T + q * U + k, k)
                for k in range(U):
                    if k < U - 1:
                        masked(b * T + (T - U) + k + 1, T - U + k + 1, k + 1, 16 * (b * Q + Q))
                    low(b * T + (T - U) + k, k)

            block_of_rows(0, True)
            with dve.Fori(1, NB) as b:
                block_of_rows(b, False)
            normalise(NB - 1)

        @block.tensor
        def _(pe):
            pe.wait_ge(ident_ready, 2)
            pe.wait_ge(wx_ready, KF * 2)

            def turn_tile(g, s, k):
                pe.wait_ge(node_ready, g * G + k + 1)
                for kf in range(KF):
                    last = nc.tensor.transpose(psum[:, k % 2, kf * P:(kf + 1) * P],
                                               node[s % 2][:, k, kf * P:(kf + 1) * P], ident[:, :])
                last.then_inc(turned, 1)

            with pe.Fori(0, NI) as i:
                for s in range(XS):
                    g = i * XS + s
                    turn_tile(g, s, 0)
                    for k in range(G):
                        if k < G - 1:
                            turn_tile(g, s, k + 1)
                        pe.wait_ge(node_t_ready, g * G + k + 1)
                        if k >= 4:
                            pe.wait_ge(h_used, g * G + k - 3)
                        for kf in range(KF):
                            last = nc.tensor.matmul(psum[:, 4 + k % 4, 0:FD], node_t[k % 2][:, kf * P:(kf + 1) * P],
                                                    wx[:, kf, :], start=(kf == 0), stop=(kf == KF - 1))
                        last.then_inc(h_ready, 1)
            pe.wait_ge(exps_ready, 3)
            nc.tensor.transpose(psum[0:T, 0, 0:P], s_cols[:, :, 0], ident[:, :]).then_inc(r_ready, 1)
            pe.wait_ge(ones_ready, 1)
            pe.wait_ge(lo_ready, T // G)

            def step(b, n, jt, k, first=False, last_step=False):
                hi, lo = (v[:, bass.ts(jt, 1), :].rearrange("p o f -> p (o f)") for v in (node_hi, node_lo))
                pe.wait_ge(p_hi_ready, n + 1)
                for it in range(TB):
                    if first:
                        pe.wait_ge(acc_free, b * TB + it + 1)
                    p = p_hi[:, k % HS, it * P:(it + 1) * P]
                    nc.tensor.matmul(psum[:, it, 0:FD], p, hi, start=first, stop=False)
                    nc.tensor.matmul(psum[:, it, 0:F], p, lo, start=False, stop=False)
                pe.wait_ge(p_lo_ready, n + 1)
                for it in range(TB):
                    mm = nc.tensor.matmul(psum[:, it, 0:FD], p_lo[:, k % LS, it * P:(it + 1) * P], hi, start=False,
                                          stop=last_step)
                    if it == TB - 1:
                        mm.then_inc(step_done, 1)
                    elif last_step:
                        mm.then_inc(acc_ready, 1)

            with pe.Fori(0, NB) as b:
                for k in range(U):
                    step(b, b * T + k, k, k, first=(k == 0))
                with pe.Fori(1, Q - 1) as q:
                    for k in range(U):
                        step(b, b * T + q * U + k, q * U + k, k)
                for k in range(U):
                    step(b, b * T + (T - U) + k, T - U + k, k, last_step=(k == U - 1))


def kernel(x, adj, L0_gnn_W, L0_gnn_a):
    import numpy as np
    import concourse.bacc as bacc
    from concourse.bass_utils import run_bass_kernel_spmd

    nodes, feats = x.shape
    block_rows = 1024
    nb, t = nodes // block_rows, nodes // P
    arrays = {
        "x": np.ascontiguousarray(x),
        "adj_t": np.ascontiguousarray(np.asarray(adj).reshape(nb, block_rows, t, P).transpose(0, 2, 3, 1)),
        "w": np.ascontiguousarray(L0_gnn_W),
        "a": np.ascontiguousarray(L0_gnn_a),
    }
    nc = bacc.Bacc("TRN2", target_bir_lowering=False, num_devices=1)
    args = [nc.dram_tensor(name, v.shape, mybir.dt.from_np(v.dtype), kind="ExternalInput").ap()
            for name, v in arrays.items()]
    out = nc.dram_tensor("out", (nodes, feats), F32, kind="ExternalOutput").ap()
    gat_layer(nc, *args, out)
    r = run_bass_kernel_spmd(nc, [arrays], core_ids=[0])
    return r.results[0]["out"]
```

```python
from contextlib import ExitStack

import concourse.bass as bass
from concourse import mybir

P = 128
EPS = 1e-5
SLOPE = 0.01
TINY = 1e-30
ALU = mybir.AluOpType
ACT = mybir.ActivationFunctionType
AX_X = mybir.AxisListType.X
F32 = mybir.dt.float32
F32R = mybir.dt.float32r
I32 = mybir.dt.int32


def gat_layer(nc: bass.Bass, x: bass.AP, adj_t: bass.AP, w: bass.AP, a: bass.AP, out: bass.AP):
    N, F = x.shape
    T = N // P
    NB, _, _, IB = adj_t.shape
    TB = IB // P
    FD = F + 2
    KF = F // P
    G = 4
    XS = 4
    NG = T // G
    NI = NG // XS
    PG = G // 2
    U = 8
    Q = T // U
    HS = 4
    LS = 2
    assert TB == 8 and G * F == IB and PG == 2 and NI >= 3 and Q >= 3

    x_t = x.rearrange("(t p) f -> p t f", p=P)
    out_t = out.rearrange("(t p) f -> p t f", p=P)
    adj_flat = adj_t.rearrange("b t p i -> p (b t) i")
    r_dram = nc.dram_tensor("r_rows", [T, P], F32, kind="Internal").ap()

    with ExitStack() as ctx:
        def sb(name, shape, dt):
            return ctx.enter_context(nc.sbuf_tensor(name, shape, dt))

        def sem(name):
            return ctx.enter_context(nc.semaphore(name))

        node_hi = sb("node_hi", [P, T, FD], F32R)
        node_lo = sb("node_lo", [P, T, F], F32R)
        ring = sb("ring", [P, U, IB], I32)
        w_buf = sb("w_buf", [P, LS, IB], F32)
        p_hi = sb("p_hi", [P, HS, IB], F32R)
        p_lo = sb("p_lo", [P, LS, IB], F32R)
        r_buf = sb("r_buf", [P, 2, IB], F32)
        wx = sb("wx", [P, KF, FD], F32)
        acc = sb("acc", [P, TB, FD], F32)
        f1 = sb("f1", [P, T], F32)
        f2 = sb("f2", [P, T], F32)
        neg_f1 = sb("neg_f1", [P, T], F32)
        s_cols = sb("s_cols", [P, T, 2], F32)
        tmp = sb("tmp", [P, 2, T], F32)
        ident = sb("ident", [P, P], F32)
        s2_max = sb("s2_max", [P, 2], F32)
        stats = sb("stats", [P, G, 6], F32)
        rstd = sb("rstd", [P, 2, G], F32)
        shift = sb("shift", [P, 2, G], F32)
        nrm = sb("nrm", [P, 8, G], F32)
        denom = sb("denom", [P, 2, TB], F32)
        psum = ctx.enter_context(nc.psum_tensor("psum", [P, 8, 512], F32))

        ring_f = ring[:, :, :].bitcast(F32)
        ones = node_hi[:, :, F:FD]
        xg = [ring_f[:, s, :].rearrange("p (k f) -> p k f", f=F) for s in range(XS)]
        node = [w_buf[:, 0, :].rearrange("p (k f) -> p k f", f=F), w_buf[:, 1, :].rearrange("p (k f) -> p k f", f=F),
                acc[:, 0:G, 0:F], acc[:, G:2 * G, 0:F]]
        node_t = [r_buf[:, 0, 0:2 * F], r_buf[:, 0, 2 * F:4 * F]]
        a_row = r_buf[:, 1, 0:2 * F].rearrange("p (s f) -> p s f", s=2)
        products = r_buf[:, 0, :].rearrange("p (n f) -> p n f", f=F)
        r_turned = r_buf[0:T, 1, 0:P]
        r_cols = tmp[:, 1, :]
        mean_diff, mean_sum, squares, square_diff, var_eps, std, rs0, newton = (nrm[:, n, :] for n in range(8))
        s1, s2 = s_cols[:, :, 0], s_cols[:, :, 1]

        x_loaded = [sem(f"x_loaded{s}") for s in range(XS)]
        xh_stored = [sem(f"xh_stored{s}") for s in range(XS)]
        weights_loaded = sem("weights_loaded")
        ident_ready = sem("ident_ready")
        ones_ready = sem("ones_ready")
        wx_ready = sem("wx_ready")
        stats_done = sem("stats_done")
        moments_done = sem("moments_done")
        var_ready = sem("var_ready")
        std_ready = sem("std_ready")
        newton_done = sem("newton_done")
        norm_ready = sem("norm_ready")
        node_ready = sem("node_ready")
        hi_ready = sem("hi_ready")
        lo_ready = sem("lo_ready")
        turned = sem("turned")
        node_t_ready = sem("node_t_ready")
        h_ready = sem("h_ready")
        h_used = sem("h_used")
        s2_max_ready = sem("s2_max_ready")
        c_ready = sem("c_ready")
        arguments_ready = sem("arguments_ready")
        exps_ready = sem("exps_ready")
        factors_ready = sem("factors_ready")
        r_ready = sem("r_ready")
        row_loaded = [sem(f"row_loaded{slot}") for slot in range(2)]
        adj_loaded = [sem(f"adj_loaded{u}") for u in range(U // 2)]
        w_ready = sem("w_ready")
        t_ready = sem("t_ready")
        p_hi_ready = sem("p_hi_ready")
        p_lo_ready = sem("p_lo_ready")
        step_done = sem("step_done")
        acc_ready = sem("acc_ready")
        acc_free = sem("acc_free")
        denom_done = sem("denom_done")
        scaled = sem("scaled")
        acc_stored = sem("acc_stored")

        block = ctx.enter_context(nc.Block())

        @block.sync
        def _(sp):
            sp.dma_start(wx[:, :, 0:F], w.rearrange("(k p) n -> p k n", p=P)).then_inc(weights_loaded, 16)
            sp.dma_start(a_row, a.rearrange("(s n) o -> (s n o)", s=2).partition_broadcast(P)
                         .rearrange("p (s n) -> p s n", s=2)).then_inc(weights_loaded, 16)
            for s in range(XS):
                sp.dma_start(xg[s], x_t[:, s * G:(s + 1) * G, :]).then_inc(x_loaded[s], 16)
            for u in range(XS // 2, U // 2):
                sp.dma_start(ring[:, 2 * u:2 * u + 2, :], adj_flat[:, 2 * u:2 * u + 2, :]).then_inc(adj_loaded[u], 16)

            def store_xh(g, s):
                sp.wait_ge(h_used, 2 + (g + 1) * PG)
                sp.dma_start(out_t[:, bass.ts(g, G), :], xg[s]).then_inc(xh_stored[s], 16)

            with sp.Fori(0, NI - 1) as i:
                for s in range(XS):
                    store_xh(i * XS + s, s)
                    sp.wait_ge(xh_stored[s], 16 * (i + 1))
                    sp.dma_start(xg[s], x_t[:, bass.ts((i + 1) * XS + s, G), :]).then_inc(x_loaded[s], 16)
            for s in range(XS):
                store_xh((NI - 1) * XS + s, s)
            for u in range(XS // 2):
                for s in (2 * u, 2 * u + 1):
                    sp.wait_ge(xh_stored[s], 16 * NI)
                sp.dma_start(ring[:, 2 * u:2 * u + 2, :], adj_flat[:, 2 * u:2 * u + 2, :]).then_inc(adj_loaded[u], 16)
            with sp.Fori(1, NB * Q) as n:
                for u in range(U // 2):
                    sp.wait_ge(p_lo_ready, n * U + (2 * u + 2 - U))
                    sp.dma_start(ring[:, 2 * u:2 * u + 2, :],
                                 adj_flat[:, bass.ts(n * (U // 2) + u, 2), :]).then_inc(adj_loaded[u], 16)

        @block.gpsimd
        def _(pool):
            nc.gpsimd.memset(ident[:, :], 0.0).then_inc(ident_ready, 1)
            pool.wait_ge(ident_ready, 1)
            nc.gpsimd.affine_select(out=ident[:, :], in_=ident[:, :], compare_op=ALU.not_equal, fill=1.0, base=0,
                                    pattern=[[-1, P]], channel_multiplier=1).then_inc(ident_ready, 1)
            nc.gpsimd.memset(ones.bitcast(F32), 1.0).then_inc(ones_ready, 1)

            def low_node(g, s):
                pool.wait_ge(hi_ready, g + 1)
                pool.wait_ge(ones_ready, 1)
                nc.gpsimd.tensor_tensor(node_lo[:, bass.ts(g, G), :], node[s],
                                        node_hi[:, bass.ts(g, G), 0:F].bitcast(F32), ALU.subtract).then_inc(lo_ready, 1)

            with pool.Fori(0, NI) as i:
                for s in range(XS):
                    low_node(i * XS + s, s)
            pool.wait_ge(s2_max_ready, 1)
            nc.gpsimd.partition_all_reduce(s2_max[:, 1:2], s2_max[:, 0:1], P, bass.bass_isa.ReduceOp.max)\
                .then_inc(c_ready, 1)

            def load_row(b, slot):
                pool.dma_start(r_buf[:, slot, :], r_dram.rearrange("t p -> (t p)")[bass.ts(b, IB)].partition_broadcast(P))\
                    .then_inc(row_loaded[slot], 16)

            def add_out(b):
                pool.wait_ge(scaled, b + 1)
                pool.dma_start(out_t[:, bass.ts(b, TB), :], acc[:, :, 0:F], accum_op=ALU.add).then_inc(acc_stored, 16)

            pool.wait_ge(acc_free, TB)
            pool.dma_start(r_dram, r_turned).then_inc(acc_stored, 16)
            pool.wait_ge(acc_stored, 16)
            load_row(0, 0)
            load_row(1, 1)
            for s in range(XS):
                pool.wait_ge(xh_stored[s], 16 * NI)
            with pool.Fori(0, NB // 2 - 1) as i:
                for slot in range(2):
                    pool.wait_ge(w_ready, (2 * i + slot + 1) * T)
                    load_row(2 * i + slot + 2, slot)
                    add_out(2 * i + slot)
            add_out(NB - 2)
            add_out(NB - 1)
            pool.wait_ge(acc_stored, 16 * (NB + 1))

        @block.scalar
        def _(act):
            def root(g):
                act.wait_ge(var_ready, g + 1)
                nc.scalar.activation(std, var_eps, ACT.Sqrt).then_inc(std_ready, 1)

            def nodes(g, s):
                act.wait_ge(norm_ready, g + 1)
                for k in range(G):
                    nc.scalar.activation(node[s][:, k, :], xg[s][:, k, :], ACT.Relu, bias=shift[:, s % 2, k:k + 1],
                                         scale=rstd[:, s % 2, k:k + 1]).then_inc(node_ready, 1)

            def high_node(g, s):
                act.wait_ge(node_ready, (g + 1) * G)
                nc.scalar.activation(node_hi[:, bass.ts(g, G), 0:F], node[s], ACT.Copy).then_inc(hi_ready, 1)

            def copy_turned(g, pair):
                act.wait_ge(turned, g * PG + pair + 1)
                nc.scalar.activation(node_t[pair], psum[:, pair, :], ACT.Copy).then_inc(node_t_ready, 1)

            def group(g, s, ahead):
                copy_turned(g, 0)
                if ahead >= 1:
                    act.wait_ge(lo_ready, g)
                    nodes(g + 1, (s + 1) % XS)
                if ahead >= 2:
                    root(g + 2)
                copy_turned(g, 1)
                if ahead >= 1:
                    high_node(g + 1, (s + 1) % XS)

            act.wait_ge(wx_ready, KF * 2)
            root(0)
            nodes(0, 0)
            high_node(0, 0)
            root(1)
            act.wait_ge(lo_ready, 1)
            with act.Fori(0, NI - 1) as i:
                for s in range(XS):
                    group(i * XS + s, s, 2)
            for s in range(XS):
                group((NI - 1) * XS + s, s, XS - 1 - s)
            act.wait_ge(arguments_ready, 2)
            nc.scalar.activation(f1[:, :], tmp[:, 0, :], ACT.Exp).then_inc(exps_ready, 1)
            nc.scalar.activation(f2[:, :], tmp[:, 0, :], ACT.Exp, scale=SLOPE).then_inc(exps_ready, 1)
            nc.scalar.activation(r_cols, r_cols, ACT.Exp, scale=SLOPE - 1.0).then_inc(exps_ready, 1)
            act.wait_ge(factors_ready, 3)

            def weights(step, jt, k, row, free=True):
                if free:
                    act.wait_ge(t_ready, step - 1)
                nc.scalar.activation(w_buf[:, k % LS, :], r_buf[:, row, :], ACT.Relu, bias=neg_f1[:, bass.ts(jt, 1)],
                                     scale=f2[:, bass.ts(jt, 1)]).then_inc(w_ready, 1)

            def high(step, k, free=True):
                act.wait_ge(t_ready, step + 1)
                if free:
                    act.wait_ge(step_done, step - (HS - 1))
                nc.scalar.activation(p_hi[:, k % HS, :], ring_f[:, k, :], ACT.Relu).then_inc(p_hi_ready, 1)

            def take_out(b):
                for it in range(TB):
                    if it < TB - 1:
                        act.wait_ge(acc_ready, b * (TB - 1) + it + 1)
                    else:
                        act.wait_ge(step_done, (b + 1) * T)
                    if it == 0:
                        act.wait_ge(acc_stored, 16 * (b + 1))
                    nc.scalar.activation(acc[:, it, :], psum[:, it, 0:FD], ACT.Copy).then_inc(acc_free, 1)

            def block_of_rows(b, row, first=False):
                act.wait_ge(row_loaded[row], (b // 2 + 1) * 16 if first else (b - row + 2) * 8)
                weights(b * T, 0, 0, row, not first)
                for k in range(U):
                    weights(b * T + k + 1, k + 1, k + 1, row, not first or k >= 1)
                    high(b * T + k, k, not first or k >= HS)
                    if k == 1 and not first:
                        take_out(b - 1)
                with act.Fori(1, Q - 1) as q:
                    for k in range(U):
                        weights(b * T + q * U + k + 1, q * U + k + 1, k + 1, row)
                        high(b * T + q * U + k, k)
                for k in range(U):
                    if k < U - 1:
                        weights(b * T + (T - U) + k + 1, T - U + k + 1, k + 1, row)
                    high(b * T + (T - U) + k, k)

            block_of_rows(0, 0, first=True)
            block_of_rows(1, 1)
            with act.Fori(1, NB // 2) as i:
                block_of_rows(i * 2, 0)
                block_of_rows(i * 2 + 1, 1)
            take_out(NB - 1)

        @block.vector
        def _(dve):
            dve.wait_ge(weights_loaded, 32)
            for k in range(KF):
                for s in range(2):
                    nc.vector.tensor_tensor_reduce(out=products[:, 2 * k + s, :], in0=wx[:, k, 0:F], in1=a_row[:, s, :], scale=1.0,
                                                   scalar=0.0, op0=ALU.mult, op1=ALU.add,
                                                   accum_out=wx[:, k, F + s:F + s + 1]).then_inc(wx_ready, 1)
            nc.vector.memset(s2_max[:, :], 0.0).then_inc(h_used, 2)

            def variance(g, s, loaded):
                dve.wait_ge(x_loaded[s], loaded)
                for k in range(G):
                    last = nc.vector.bn_stats(stats[:, k, :], xg[s][:, k, :])
                last.then_inc(stats_done, 1)
                dve.wait_ge(stats_done, g + 1)
                nc.vector.tensor_tensor(mean_diff, stats[:, :, 1], stats[:, :, 4], ALU.subtract)
                nc.vector.tensor_tensor(mean_sum, stats[:, :, 1], stats[:, :, 4], ALU.add)
                nc.vector.tensor_tensor(squares, stats[:, :, 2], stats[:, :, 5], ALU.add).then_inc(moments_done, 1)
                dve.wait_ge(moments_done, g * 2 + 1)
                nc.vector.scalar_tensor_tensor(out=square_diff, in0=mean_diff, scalar=0.25, in1=mean_diff,
                                               op0=ALU.mult, op1=ALU.mult)
                nc.vector.tensor_scalar(squares, squares, 1.0 / F, EPS, ALU.mult, ALU.add).then_inc(moments_done, 1)
                dve.wait_ge(moments_done, g * 2 + 2)
                nc.vector.tensor_tensor(var_eps, squares, square_diff, ALU.add).then_inc(var_ready, 1)

            def scales(g, s):
                dve.wait_ge(std_ready, g + 1)
                nc.vector.reciprocal(rs0, std).then_inc(newton_done, 1)
                dve.wait_ge(newton_done, g * 4 + 1)
                nc.vector.scalar_tensor_tensor(out=newton, in0=rs0, scalar=-0.5, in1=rs0, op0=ALU.mult,
                                               op1=ALU.mult).then_inc(newton_done, 1)
                dve.wait_ge(newton_done, g * 4 + 2)
                nc.vector.tensor_tensor(newton, newton, var_eps, ALU.mult).then_inc(newton_done, 1)
                dve.wait_ge(newton_done, g * 4 + 3)
                nc.vector.scalar_tensor_tensor(out=rstd[:, s % 2, :], in0=newton, scalar=1.5, in1=rs0, op0=ALU.add,
                                               op1=ALU.mult).then_inc(newton_done, 1)
                dve.wait_ge(newton_done, g * 4 + 4)
                nc.vector.scalar_tensor_tensor(out=shift[:, s % 2, :], in0=mean_sum, scalar=-0.5,
                                               in1=rstd[:, s % 2, :], op0=ALU.mult, op1=ALU.mult)\
                    .then_inc(norm_ready, 1)

            def take_h(g, s, pair):
                banks = slice(4 + 2 * pair, 6 + 2 * pair)
                dve.wait_ge(h_ready, g * PG + pair + 1)
                nc.vector.tensor_copy(s_cols[:, bass.ts(g * PG + pair, 2), :], psum[:, banks, F:FD])
                nc.vector.tensor_tensor(xg[s][:, 2 * pair:2 * pair + 2, :], psum[:, banks, 0:F],
                                        xg[s][:, 2 * pair:2 * pair + 2, :], ALU.add).then_inc(h_used, 1)

            variance(0, 0, 16)
            scales(0, 0)
            variance(1, 1, 16)
            scales(1, 1)
            with dve.Fori(0, NI - 1) as i:
                for s in range(XS):
                    variance(i * XS + s + 2, (s + 2) % XS, 16 * (i + (1 if s + 2 < XS else 2)))
                    take_h(i * XS + s, s, 0)
                    scales(i * XS + s + 2, (s + 2) % XS)
                    take_h(i * XS + s, s, 1)
            for s in range(XS):
                g = (NI - 1) * XS + s
                if s + 2 < XS:
                    variance(g + 2, s + 2, 16 * NI)
                take_h(g, s, 0)
                if s + 2 < XS:
                    scales(g + 2, s + 2)
                take_h(g, s, 1)
            dve.wait_ge(h_used, 2 + NG * PG)
            nc.vector.tensor_reduce(s2_max[:, 0:1], s2, AX_X, ALU.max).then_inc(s2_max_ready, 1)
            dve.wait_ge(c_ready, 1)
            nc.vector.tensor_scalar(tmp[:, 0, :], s2, s2_max[:, 1:2], None, ALU.subtract).then_inc(arguments_ready, 1)
            nc.vector.tensor_scalar(tmp[:, 1, :], s1, s2_max[:, 1:2], 0.0, ALU.add, ALU.max)\
                .then_inc(arguments_ready, 1)
            dve.wait_ge(exps_ready, 3)
            nc.vector.tensor_scalar(neg_f1[:, :], f1[:, :], -0.5, None, ALU.mult).then_inc(factors_ready, 1)
            nc.vector.tensor_scalar(f2[:, :], f2[:, :], 0.5, None, ALU.mult).then_inc(factors_ready, 1)
            nc.vector.tensor_scalar(f1[:, :], f1[:, :], 0.5, None, ALU.mult).then_inc(factors_ready, 1)
            dve.wait_ge(r_ready, 1)
            nc.vector.tensor_copy(r_turned, psum[0:T, 0, 0:P]).then_inc(acc_free, TB)
            dve.wait_ge(factors_ready, 3)

            def masked(step, jt, k, loaded):
                dve.wait_ge(w_ready, step + 1)
                if k % 2 == 0:
                    dve.wait_ge(adj_loaded[k // 2], loaded)
                nc.vector.scalar_tensor_tensor(out=ring_f[:, k, :], in0=w_buf[:, k % LS, :],
                                               scalar=f1[:, bass.ts(jt, 1)], in1=ring[:, k, :], op0=ALU.add,
                                               op1=ALU.min).then_inc(t_ready, 1)

            def low(step, k, free=True):
                dve.wait_ge(p_hi_ready, step + 1)
                if free:
                    dve.wait_ge(step_done, step - (LS - 1))
                nc.vector.scalar_tensor_tensor(out=p_lo[:, k % LS, :], in0=ring_f[:, k, :], scalar=0.0,
                                               in1=p_hi[:, k % HS, :].bitcast(F32), op0=ALU.max, op1=ALU.subtract)\
                    .then_inc(p_lo_ready, 1)

            def normalise(b):
                dve.wait_ge(acc_free, (b + 2) * TB)
                nc.vector.tensor_scalar(denom[:, 0, :], acc[:, :, F], TINY, None, ALU.max).then_inc(denom_done, 1)
                dve.wait_ge(denom_done, 2 * b + 1)
                nc.vector.reciprocal(denom[:, 1, :], denom[:, 0, :]).then_inc(denom_done, 1)
                dve.wait_ge(denom_done, 2 * b + 2)
                for it in range(TB):
                    last = nc.vector.tensor_scalar(acc[:, it, 0:F], acc[:, it, 0:F], denom[:, 1, it:it + 1], None,
                                                   ALU.mult)
                last.then_inc(scaled, 1)

            def block_of_rows(b, first):
                masked(b * T, 0, 0, 16 * (b * Q + 1))
                for k in range(U):
                    turn = b * Q + (2 if k == U - 1 else 1)
                    masked(b * T + k + 1, k + 1, (k + 1) % U, 16 * turn)
                    low(b * T + k, k, not first or k >= LS)
                    if k == 3 and not first:
                        normalise(b - 1)
                with dve.Fori(1, Q - 1) as q:
                    for k in range(U):
                        turn = b * Q + q + (2 if k == U - 1 else 1)
                        masked(b * T + q * U + k + 1, q * U + k + 1, (k + 1) % U, 16 * turn)
                        low(b * T + q * U + k, k)
                for k in range(U):
                    if k < U - 1:
                        masked(b * T + (T - U) + k + 1, T - U + k + 1, k + 1, 16 * (b * Q + Q))
                    low(b * T + (T - U) + k, k)

            block_of_rows(0, True)
            with dve.Fori(1, NB) as b:
                block_of_rows(b, False)
            normalise(NB - 1)

        @block.tensor
        def _(pe):
            pe.wait_ge(ident_ready, 2)
            pe.wait_ge(wx_ready, KF * 2)

            def turn_pair(g, s, pair):
                pe.wait_ge(node_ready, g * G + 2 * pair + 2)
                for n in range(2 * KF):
                    k, kf = 2 * pair + n // KF, n % KF
                    last = nc.tensor.transpose(psum[:, pair, n * P:(n + 1) * P], node[s][:, k, kf * P:(kf + 1) * P],
                                               ident[:, :])
                last.then_inc(turned, 1)

            def product(g, pair):
                pe.wait_ge(node_t_ready, g * PG + pair + 1)
                pe.wait_ge(h_used, g * PG + pair + 1)
                for n in range(2 * KF):
                    k, kf = n // KF, n % KF
                    last = nc.tensor.matmul(psum[:, 4 + 2 * pair + k, 0:FD], node_t[pair][:, n * P:(n + 1) * P],
                                            wx[:, kf, :], start=(kf == 0), stop=(kf == KF - 1))
                last.then_inc(h_ready, 1)

            turn_pair(0, 0, 0)
            with pe.Fori(0, NI - 1) as i:
                for s in range(XS):
                    turn_pair(i * XS + s, s, 1)
                    product(i * XS + s, 0)
                    turn_pair(i * XS + s + 1, (s + 1) % XS, 0)
                    product(i * XS + s, 1)
            for s in range(XS):
                g = (NI - 1) * XS + s
                turn_pair(g, s, 1)
                product(g, 0)
                if s + 1 < XS:
                    turn_pair(g + 1, s + 1, 0)
                product(g, 1)
            pe.wait_ge(exps_ready, 3)
            nc.tensor.transpose(psum[0:T, 0, 0:P], r_cols, ident[:, :]).then_inc(r_ready, 1)
            pe.wait_ge(ones_ready, 1)
            pe.wait_ge(lo_ready, NG)

            def step(b, n, jt, k, first=False, last=False):
                hi, lo = (v[:, bass.ts(jt, 1), :].rearrange("p o f -> p (o f)") for v in (node_hi, node_lo))

                def high_products(it):
                    if first:
                        pe.wait_ge(acc_free, b * TB + it + 1)
                    p = p_hi[:, k % HS, it * P:(it + 1) * P]
                    nc.tensor.matmul(psum[:, it, 0:FD], p, hi, start=first, stop=False)
                    nc.tensor.matmul(psum[:, it, 0:F], p, lo, start=False, stop=False)

                def low_product(it):
                    return nc.tensor.matmul(psum[:, it, 0:FD], p_lo[:, k % LS, it * P:(it + 1) * P], hi, start=False,
                                            stop=last)

                pe.wait_ge(p_hi_ready, n + 1)
                if last:
                    pe.wait_ge(p_lo_ready, n + 1)
                    for it in range(TB):
                        high_products(it)
                        low_product(it).then_inc(acc_ready if it < TB - 1 else step_done, 1)
                    return
                for it in range(TB):
                    high_products(it)
                pe.wait_ge(p_lo_ready, n + 1)
                for it in range(TB):
                    mm = low_product(it)
                mm.then_inc(step_done, 1)

            with pe.Fori(0, NB) as b:
                for k in range(U):
                    step(b, b * T + k, k, k, first=(k == 0))
                with pe.Fori(1, Q - 1) as q:
                    for k in range(U):
                        step(b, b * T + q * U + k, q * U + k, k)
                for k in range(U):
                    step(b, b * T + (T - U) + k, T - U + k, k, last=(k == U - 1))


def kernel(x, adj, L0_gnn_W, L0_gnn_a):
    import numpy as np
    import concourse.bacc as bacc
    from concourse.bass_utils import run_bass_kernel_spmd

    nodes, feats = x.shape
    block_rows = 1024
    nb, t = nodes // block_rows, nodes // P
    arrays = {
        "x": np.ascontiguousarray(x),
        "adj_t": np.ascontiguousarray(np.asarray(adj).reshape(nb, block_rows, t, P).transpose(0, 2, 3, 1)),
        "w": np.ascontiguousarray(L0_gnn_W),
        "a": np.ascontiguousarray(L0_gnn_a),
    }
    nc = bacc.Bacc("TRN2", target_bir_lowering=False, num_devices=1, dynamic_dma_scratch_size=8192)
    args = [nc.dram_tensor(name, v.shape, mybir.dt.from_np(v.dtype), kind="ExternalInput").ap()
            for name, v in arrays.items()]
    out = nc.dram_tensor("out", (nodes, feats), F32, kind="ExternalOutput").ap()
    gat_layer(nc, *args, out)
    r = run_bass_kernel_spmd(nc, [arrays], core_ids=[0])
    return r.results[0]["out"]
```

```python
from contextlib import ExitStack

import concourse.bass as bass
from concourse import mybir

P = 128
EPS = 1e-5
SLOPE = 0.01
TINY = 1e-30
LOWEST_SUM = 2.0 ** -70
NO_EDGE = -1e38
ALU = mybir.AluOpType
ACT = mybir.ActivationFunctionType
AX_X = mybir.AxisListType.X
F32 = mybir.dt.float32
F32R = mybir.dt.float32r
I32 = mybir.dt.int32


def gat_layer(nc: bass.Bass, x: bass.AP, adj_t: bass.AP, w: bass.AP, a: bass.AP, out: bass.AP):
    N, F = x.shape
    T = N // P
    NB, _, _, IB = adj_t.shape
    TB = IB // P
    FD = F + 2
    KF = F // P
    G = 4
    XS = 4
    NG = T // G
    NI = NG // XS
    PG = G // 2
    U = 8
    Q = T // U
    HS = 4
    LS = 2
    NP = T // 2
    assert TB == 8 and G * F == IB and PG == 2 and NI >= 3 and Q >= 3

    x_t = x.rearrange("(t p) f -> p t f", p=P)
    out_t = out.rearrange("(t p) f -> p t f", p=P)
    adj_flat = adj_t.rearrange("b t p i -> p (b t) i")
    s1_dram = nc.dram_tensor("s1_rows", [T, P], F32, kind="Internal").ap()
    r_dram = nc.dram_tensor("r_rows", [T, P], F32, kind="Internal").ap()

    with ExitStack() as ctx:
        def sb(name, shape, dt):
            return ctx.enter_context(nc.sbuf_tensor(name, shape, dt))

        def sem(name):
            return ctx.enter_context(nc.semaphore(name))

        node_hi = sb("node_hi", [P, T, FD], F32R)
        with nc.sbuf_tensor("x_sb", [P, T, F], F32) as x_sb:
            pass
        node_lo = sb("node_lo", [P, T, F], F32R)
        ring = sb("ring", [P, U, IB], I32)
        w_buf = sb("w_buf", [P, LS, IB], F32)
        p_hi = sb("p_hi", [P, HS, IB], F32R)
        p_lo = sb("p_lo", [P, LS, IB], F32R)
        r_buf = sb("r_buf", [P, 2, IB], F32)
        wx = sb("wx", [P, KF, FD], F32)
        acc = sb("acc", [P, TB, FD], F32)
        f1 = sb("f1", [P, T], F32)
        f2 = sb("f2", [P, T], F32)
        neg_f1 = sb("neg_f1", [P, T], F32)
        s_cols = sb("s_cols", [P, T, 2], F32)
        tmp = sb("tmp", [P, 2, T], F32)
        ident = sb("ident", [P, P], F32)
        s2_max = sb("s2_max", [P, 2], F32)
        stats = sb("stats", [P, G, 6], F32)
        rstd = sb("rstd", [P, XS, G], F32)
        shift = sb("shift", [P, XS, G], F32)
        nrm = sb("nrm", [P, 5, G], F32)
        mean_sum = sb("mean_sum", [P, 2, G], F32)
        var_eps = sb("var_eps", [P, 2, G], F32)
        std = sb("std", [P, 2, G], F32)
        denom = sb("denom", [P, 2, TB], F32)
        lowest = sb("lowest", [P, TB], F32)
        too_low = sb("too_low", [P, 2], F32)
        second_pass = sb("second_pass", [P, 1], I32)
        psum = ctx.enter_context(nc.psum_tensor("psum", [P, 8, 512], F32))

        ring_f = ring[:, :, :].bitcast(F32)
        ones = node_hi[:, :, F:FD]
        xh_dram = nc.dram_tensor("x_plus_hw", [N, F], F32, kind="Internal").ap().rearrange("(t p) f -> p t f", p=P)
        xh = [ring_f[:, U - XS + s, :].rearrange("p (k f) -> p k f", f=F) for s in range(XS)]
        node = [w_buf[:, 0, :].rearrange("p (k f) -> p k f", f=F), w_buf[:, 1, :].rearrange("p (k f) -> p k f", f=F),
                acc[:, 0:G, 0:F], acc[:, G:2 * G, 0:F]]
        node_t = [r_buf[:, 0, 0:2 * F], r_buf[:, 0, 2 * F:4 * F]]
        a_row = r_buf[:, 1, 0:2 * F].rearrange("p (s f) -> p s f", s=2)
        products = r_buf[:, 0, :].rearrange("p (n f) -> p n f", f=F)
        r_turned = r_buf[0:T, 1, 0:P]
        r_cols = tmp[:, 1, :]
        mean_diff, squares, square_diff, rs0, newton = (nrm[:, n, :] for n in range(5))
        s1, s2 = s_cols[:, :, 0], s_cols[:, :, 1]
        row_max, work, work2, weights2 = (ring_f[:, 2 + n, :] for n in range(4))
        xh_rows = ring_f[:, 6:8, :].rearrange("p s (k f) -> p (s k) f", f=F)
        gate, exps = w_buf[:, 0, :], w_buf[:, 1, :]
        s1_row, top_row = r_buf[:, 0, :], r_buf[:, 1, :]
        ones_square = p_hi[:, HS - 1, 0:P]
        node_sums = wx[:, 0, 0:F]

        x_loaded = [sem(f"x_loaded{s}") for s in range(XS)]
        xh_stored = [sem(f"xh_stored{s}") for s in range(XS)]
        weights_loaded = sem("weights_loaded")
        ident_ready = sem("ident_ready")
        ones_ready = sem("ones_ready")
        wx_ready = sem("wx_ready")
        stats_done = sem("stats_done")
        moments_done = sem("moments_done")
        var_ready = sem("var_ready")
        std_ready = sem("std_ready")
        newton_done = sem("newton_done")
        norm_ready = sem("norm_ready")
        node_ready = sem("node_ready")
        hi_ready = sem("hi_ready")
        lo_ready = sem("lo_ready")
        turned = sem("turned")
        node_t_ready = sem("node_t_ready")
        h_ready = sem("h_ready")
        s_ready = sem("s_ready")
        h_used = sem("h_used")
        s2_max_ready = sem("s2_max_ready")
        c_ready = sem("c_ready")
        arguments_ready = sem("arguments_ready")
        exps_ready = sem("exps_ready")
        factors_ready = sem("factors_ready")
        r_ready = sem("r_ready")
        first_w_ready = sem("first_w_ready")
        first_t_ready = sem("first_t_ready")
        half_hi_ready = sem("half_hi_ready")
        row_loaded = [sem(f"row_loaded{slot}") for slot in range(2)]
        adj_loaded = [sem(f"adj_loaded{u}") for u in range(U // 2)]
        w_ready = sem("w_ready")
        t_ready = sem("t_ready")
        p_hi_ready = sem("p_hi_ready")
        p_lo_ready = sem("p_lo_ready")
        step_done = sem("step_done")
        acc_ready = sem("acc_ready")
        acc_free = sem("acc_free")
        denom_done = sem("denom_done")
        scaled = sem("scaled")
        acc_stored = sem("acc_stored")
        odd_scaled = sem("odd_scaled")
        lowest_done = sem("lowest_done")
        too_low_ready = sem("too_low_ready")
        second_pass_ready = sem("second_pass_ready")
        rows_stored = sem("rows_stored")
        ones_square_ready = sem("ones_square_ready")
        s1_row_loaded = sem("s1_row_loaded")
        xh_rows_loaded = sem("xh_rows_loaded")
        pair_loaded = sem("pair_loaded")
        pair_used = sem("pair_used")
        candidates_done = sem("candidates_done")
        row_max_ready = sem("row_max_ready")
        top_done = sem("top_done")
        logits_done = sem("logits_done")
        exps_done = sem("exps_done")
        weights_done = sem("weights_done")
        weights_hi_ready = sem("weights_hi_ready")
        weights_lo_ready = sem("weights_lo_ready")
        tile_done = sem("tile_done")
        banks_taken = sem("banks_taken")
        mean_done = sem("mean_done")
        rows_ready = sem("rows_ready")

        def x_tile(t):
            return x_sb[:, bass.ds(t, 1), :].rearrange("p o f -> p (o f)")

        block = ctx.enter_context(nc.Block())

        @block.sync
        def _(sp):
            def load_x(g, s):
                sp.dma_start(x_sb[:, bass.ts(g, G), :], x_t[:, bass.ts(g, G), :]).then_inc(x_loaded[s], 16)

            load_x(0, 0)
            sp.dma_start(wx[:, :, 0:F], w.rearrange("(k p) n -> p k n", p=P)).then_inc(weights_loaded, 16)
            sp.dma_start(a_row, a.rearrange("(s n) o -> (s n o)", s=2).partition_broadcast(P)
                         .rearrange("p (s n) -> p s n", s=2)).then_inc(weights_loaded, 16)
            for s in range(1, XS):
                load_x(s, s)
            with sp.Fori(1, NI) as i:
                for s in range(XS):
                    sp.wait_ge(x_loaded[s], 16 * i)
                    load_x(i * XS + s, s)

            def load_adj(u, n=0):
                sp.dma_start(ring[:, 2 * u:2 * u + 2, :],
                             adj_flat[:, bass.ts(n * (U // 2) + u, 2), :]).then_inc(adj_loaded[u], 16)

            for u in range((U - XS) // 2):
                load_adj(u)

            def store_xh(g, s):
                sp.wait_ge(h_used, 2 + (g + 1) * PG)
                sp.dma_start(out_t[:, bass.ts(g, G), :], xh[s]).then_inc(xh_stored[s], 16)
                sp.dma_start(xh_dram[:, bass.ts(g, G), :], xh[s]).then_inc(xh_stored[s], 16)

            with sp.Fori(0, NI) as i:
                for s in range(XS):
                    store_xh(i * XS + s, s)
            for u in range((U - XS) // 2, U // 2):
                for s in (2 * u - (U - XS), 2 * u + 1 - (U - XS)):
                    sp.wait_ge(xh_stored[s], 32 * NI)
                load_adj(u)
            with sp.Fori(1, NB * Q) as n:
                for u in range(U // 2):
                    sp.wait_ge(p_lo_ready, n * U + (2 * u + 2 - U))
                    load_adj(u, n)

            sp.wait_ge(second_pass_ready, 1)
            with sp.If(sp.value_load(second_pass[0:1, 0:1]) > 0):
                sp.wait_ge(acc_stored, 16 * (NB + 2))
                sp.dma_start(s1_dram.rearrange("t p -> p t"), s1, allow_slow_non_contiguous=True)\
                    .then_inc(rows_stored, 16)
                sp.wait_ge(rows_stored, 16)
                with sp.Fori(0, NB) as b:
                    sp.dma_start(s1_row, s1_dram.rearrange("t p -> (t p)")[bass.ts(b, IB)].partition_broadcast(P))\
                        .then_inc(s1_row_loaded, 16)
                    sp.dma_start(xh_rows, xh_dram[:, bass.ts(b, TB), :]).then_inc(xh_rows_loaded, 16)
                    for half in range(2):
                        with sp.Fori(0, NP) as n:
                            sp.wait_ge(pair_used, (2 * b + half) * NP + n + 1)
                            sp.dma_start(ring[:, 0:2, :], adj_flat[:, bass.ts(b * NP + n, 2), :])\
                                .then_inc(pair_loaded, 16)
                    sp.wait_ge(rows_ready, b + 1)
                    sp.dma_start(out_t[:, bass.ts(b, TB), :], acc[:, :, 0:F]).then_inc(rows_stored, 16)
                sp.wait_ge(rows_stored, 16 * (NB + 1))

        @block.gpsimd
        def _(pool):
            nc.gpsimd.memset(ident[:, :], 0.0).then_inc(ident_ready, 1)
            pool.wait_ge(ident_ready, 1)
            nc.gpsimd.affine_select(out=ident[:, :], in_=ident[:, :], compare_op=ALU.not_equal, fill=1.0, base=0,
                                    pattern=[[-1, P]], channel_multiplier=1).then_inc(ident_ready, 1)
            nc.gpsimd.memset(ones.bitcast(F32), 1.0).then_inc(ones_ready, 1)

            def low_node(g, s):
                pool.wait_ge(hi_ready, g + 1)
                pool.wait_ge(h_used, 2 + (g + 1) * PG)
                nc.gpsimd.tensor_tensor(node_lo[:, bass.ts(g, G), :], node[s],
                                        node_hi[:, bass.ts(g, G), 0:F].bitcast(F32), ALU.subtract).then_inc(lo_ready, 1)

            with pool.Fori(0, NI - 1) as i:
                for s in range(XS):
                    low_node(i * XS + s, s)
            for s in range(XS - 1):
                low_node((NI - 1) * XS + s, s)
            pool.wait_ge(s2_max_ready, 1)
            nc.gpsimd.partition_all_reduce(s2_max[:, 1:2], s2_max[:, 0:1], P, bass.bass_isa.ReduceOp.max)\
                .then_inc(c_ready, 1)
            low_node(NG - 1, XS - 1)

            def load_row(b, slot):
                row = r_dram.rearrange("t p -> (t p)")[bass.ts(b, IB)]
                pool.dma_start(r_buf[:, slot, :], row.partition_broadcast(P)).then_inc(row_loaded[slot], 16)

            def add_out(b):
                pool.wait_ge(scaled, (b + 1) * TB)
                pool.dma_start(out_t[:, bass.ts(b, TB), :], acc[:, :, 0:F], accum_op=ALU.add).then_inc(acc_stored, 16)

            pool.wait_ge(acc_free, TB // 2)
            pool.dma_start(r_dram, r_turned).then_inc(acc_stored, 16)
            pool.wait_ge(acc_stored, 16)
            pool.wait_ge(r_ready, 3)
            load_row(1, 1)
            for s in range(XS):
                pool.wait_ge(xh_stored[s], 32 * NI)
            with pool.Fori(0, NB // 2 - 1) as i:
                for slot in range(2):
                    pool.wait_ge(w_ready, (2 * i + slot + 1) * T)
                    load_row(2 * i + slot + 2, slot)
                    add_out(2 * i + slot)
            add_out(NB - 2)
            for half in range(2):
                tiles = slice(half * TB // 2, (half + 1) * TB // 2)
                pool.wait_ge(scaled, (NB - 1) * TB + 1 + half)
                pool.wait_ge(odd_scaled, half + 1)
                pool.dma_start(out_t[:, (NB - 1) * TB + tiles.start:(NB - 1) * TB + tiles.stop, :],
                               acc[:, tiles, 0:F], accum_op=ALU.add).then_inc(acc_stored, 16)
            pool.wait_ge(lowest_done, 3)
            nc.gpsimd.partition_all_reduce(too_low[:, 1:2], too_low[:, 0:1], P, bass.bass_isa.ReduceOp.max)\
                .then_inc(too_low_ready, 1)
            pool.wait_ge(acc_stored, 16 * (NB + 2))

            pool.wait_ge(second_pass_ready, 1)
            with pool.If(pool.value_load(second_pass[0:1, 0:1]) > 0):
                with pool.Fori(0, NB) as b:
                    pool.wait_ge(candidates_done, (b + 1) * (3 * T + 1))
                    nc.gpsimd.tensor_tensor(ident[:, 0:1], ident[:, 0:1], ident[:, 1:2], ALU.add)
                    nc.gpsimd.partition_all_reduce(work2, row_max, P, bass.bass_isa.ReduceOp.max)\
                        .then_inc(row_max_ready, 1)

        @block.scalar
        def _(act):
            def root(g, s):
                act.wait_ge(var_ready, g + 1)
                nc.scalar.activation(std[:, s % 2, :], var_eps[:, s % 2, :], ACT.Sqrt).then_inc(std_ready, 1)

            def nodes(g, s, free=True):
                if free:
                    act.wait_ge(lo_ready, g - (XS - 1))
                act.wait_ge(norm_ready, g + 1)
                for k in range(G):
                    nc.scalar.activation(node[s][:, k, :], x_tile(g * G + k), ACT.Relu, bias=shift[:, s, k:k + 1],
                                         scale=rstd[:, s, k:k + 1]).then_inc(node_ready, 1)

            def high_node(g, s):
                act.wait_ge(node_ready, (g + 1) * G)
                nc.scalar.activation(node_hi[:, bass.ts(g, G), 0:F], node[s], ACT.Copy).then_inc(hi_ready, 1)

            def copy_turned(g, pair):
                act.wait_ge(turned, g * PG + pair + 1)
                nc.scalar.activation(node_t[pair], psum[:, pair, :], ACT.Copy).then_inc(node_t_ready, 1)

            def group(g, s, ahead=3, free=True, first=False):
                copy_turned(g, 0)
                if ahead >= 1:
                    nodes(g + 1, (s + 1) % XS, free)
                copy_turned(g, 1)
                if first:
                    root(2, 2)
                if ahead >= 3:
                    root(g + 3, s + 3)
                if ahead >= 1:
                    high_node(g + 1, (s + 1) % XS)

            root(0, 0)
            nodes(0, 0, False)
            root(1, 1)
            high_node(0, 0)
            act.wait_ge(wx_ready, KF * 2)
            for s in range(XS):
                group(s, s, free=(s + 1 >= XS), first=(s == 0))
            with act.Fori(1, NI - 1) as i:
                for s in range(XS):
                    group(i * XS + s, s)
            for s in range(XS):
                group((NI - 1) * XS + s, s, XS - 1 - s)
            act.wait_ge(arguments_ready, 1)
            nc.scalar.activation(r_cols, r_cols, ACT.Exp, scale=SLOPE - 1.0).then_inc(exps_ready, 1)
            act.wait_ge(arguments_ready, 2)
            nc.scalar.activation(f1[:, :], tmp[:, 0, :], ACT.Exp).then_inc(exps_ready, 1)
            nc.scalar.activation(f2[:, :], tmp[:, 0, :], ACT.Exp, scale=SLOPE).then_inc(exps_ready, 1)
            act.wait_ge(factors_ready, 3)

            def weights(step, jt, k, row, free=True):
                if free:
                    act.wait_ge(t_ready, step - 1)
                nc.scalar.activation(w_buf[:, k % LS, :], r_buf[:, row, :], ACT.Relu, bias=neg_f1[:, bass.ts(jt, 1)],
                                     scale=f2[:, bass.ts(jt, 1)]).then_inc(w_ready, 1)

            def first_weights():
                for half in range(2):
                    act.wait_ge(r_ready, 2 + half)
                    nc.scalar.activation(w_buf[:, 0, half * IB // 2:(half + 1) * IB // 2],
                                         psum[:, TB // 2 + half, :], ACT.Relu, bias=neg_f1[:, 0:1],
                                         scale=f2[:, 0:1]).then_inc(first_w_ready if half == 0 else w_ready, 1)

            def high(step, k, free=True, opens=False, first=False):
                if first:
                    act.wait_ge(first_t_ready, 1)
                else:
                    act.wait_ge(t_ready, step + 1)
                if free:
                    act.wait_ge(step_done, step - (HS - 1))
                if opens:
                    nc.scalar.activation(p_hi[:, k % HS, 0:IB // 2], ring_f[:, k, 0:IB // 2], ACT.Relu)\
                        .then_inc(half_hi_ready, 1)
                    if first:
                        act.wait_ge(t_ready, 1)
                    nc.scalar.activation(p_hi[:, k % HS, IB // 2:IB], ring_f[:, k, IB // 2:IB], ACT.Relu)\
                        .then_inc(p_hi_ready, 1)
                else:
                    nc.scalar.activation(p_hi[:, k % HS, :], ring_f[:, k, :], ACT.Relu).then_inc(p_hi_ready, 1)

            def take_out(b, banks):
                for it in banks:
                    if it < TB - 1:
                        act.wait_ge(acc_ready, b * (TB - 1) + it + 1)
                    else:
                        act.wait_ge(step_done, (b + 1) * T)
                    if it == 0:
                        act.wait_ge(acc_stored, 16 * (b + 1))
                    nc.scalar.activation(acc[:, it, :], psum[:, it, 0:FD], ACT.Copy).then_inc(acc_free, 1)

            def block_of_rows(b, row, first=False):
                if first:
                    first_weights()
                else:
                    act.wait_ge(row_loaded[row], (b + row) * 8)
                    weights(b * T, 0, 0, row)
                for k in range(U):
                    if k == 0 and first:
                        high(0, 0, False, opens=True, first=True)
                        act.wait_ge(acc_free, TB)
                    if k == 1 and not first:
                        take_out(b - 1, range(TB // 2))
                    weights(b * T + k + 1, k + 1, k + 1, row, not first or k >= 1)
                    if k == 1 and not first:
                        take_out(b - 1, range(TB // 2, TB))
                    if k > 0 or not first:
                        high(b * T + k, k, not first or k >= HS, opens=(k == 0))
                with act.Fori(1, Q - 1) as q:
                    for k in range(U):
                        weights(b * T + q * U + k + 1, q * U + k + 1, k + 1, row)
                        high(b * T + q * U + k, k)
                for k in range(U):
                    if k < U - 1:
                        weights(b * T + (T - U) + k + 1, T - U + k + 1, k + 1, row)
                    high(b * T + (T - U) + k, k)

            block_of_rows(0, 0, first=True)
            block_of_rows(1, 1)
            with act.Fori(1, NB // 2) as i:
                block_of_rows(i * 2, 0)
                block_of_rows(i * 2 + 1, 1)
            act.wait_ge(acc_stored, 16 * NB)
            for half in range(2):
                act.wait_ge(denom_done, 2 * (NB - 1) + 2 * (half + 1))
                for it in (half * (TB // 2) + 1, half * (TB // 2) + 3):
                    last = nc.scalar.activation(acc[:, it, 0:F], psum[:, it, 0:F], ACT.Copy,
                                                scale=denom[:, 1, it:it + 1])
                last.then_inc(odd_scaled, 1)

            act.wait_ge(second_pass_ready, 1)
            with act.If(act.value_load(second_pass[0:1, 0:1]) > 0):
                act.wait_ge(tile_done, 1)
                nc.scalar.activation(node_sums, psum[:, 0, 0:F], ACT.Copy).then_inc(banks_taken, 1)
                with act.Fori(0, NB) as b:
                    with act.Fori(0, T) as jt:
                        act.wait_ge(logits_done, 4 * (b * T + jt) + 4)
                        nc.scalar.activation(exps, work2, ACT.Exp).then_inc(exps_done, 1)
                        act.wait_ge(weights_done, b * T + jt + 1)
                        act.wait_ge(tile_done, b * T + jt + 1)
                        nc.scalar.activation(p_hi[:, 0, :], weights2, ACT.Copy).then_inc(weights_hi_ready, 1)
                    act.wait_ge(tile_done, (b + 1) * T + 1)
                    act.wait_ge(rows_stored, 16 * (b + 1))
                    for it in range(TB):
                        nc.scalar.activation(acc[:, it, :], psum[:, it, 0:FD], ACT.Copy).then_inc(banks_taken, 1)

        @block.vector
        def _(dve):
            nc.vector.memset(s2_max[:, :], 0.0).then_inc(h_used, 2)
            nc.vector.memset(lowest[:, :], 1.0)

            def statistics(g, k):
                return nc.vector.bn_stats(stats[:, k, :], x_tile(g * G + k))

            def variance(g, s):
                dve.wait_ge(stats_done, g + 1)
                nc.vector.tensor_tensor(mean_diff, stats[:, :, 1], stats[:, :, 4], ALU.subtract)
                nc.vector.tensor_tensor(mean_sum[:, s % 2, :], stats[:, :, 1], stats[:, :, 4], ALU.add)
                nc.vector.tensor_tensor(squares, stats[:, :, 2], stats[:, :, 5], ALU.add).then_inc(moments_done, 1)
                dve.wait_ge(moments_done, g * 2 + 1)
                nc.vector.scalar_tensor_tensor(out=square_diff, in0=mean_diff, scalar=0.25, in1=mean_diff,
                                               op0=ALU.mult, op1=ALU.mult)
                nc.vector.tensor_scalar(squares, squares, 1.0 / F, EPS, ALU.mult, ALU.add).then_inc(moments_done, 1)
                dve.wait_ge(moments_done, g * 2 + 2)
                nc.vector.tensor_tensor(var_eps[:, s % 2, :], squares, square_diff, ALU.add).then_inc(var_ready, 1)

            def statistics_and_variance(g, s):
                dve.wait_ge(x_loaded[s], 16)
                for k in range(G):
                    last = statistics(g, k)
                last.then_inc(stats_done, 1)
                variance(g, s)

            def scale_step(g, s, n):
                if n == 0:
                    dve.wait_ge(std_ready, g + 1)
                    nc.vector.reciprocal(rs0, std[:, s % 2, :]).then_inc(newton_done, 1)
                elif n == 1:
                    dve.wait_ge(newton_done, g * 4 + 1)
                    nc.vector.scalar_tensor_tensor(out=newton, in0=rs0, scalar=-0.5, in1=rs0, op0=ALU.mult,
                                                   op1=ALU.mult).then_inc(newton_done, 1)
                elif n == 2:
                    dve.wait_ge(newton_done, g * 4 + 2)
                    nc.vector.tensor_tensor(newton, newton, var_eps[:, s % 2, :], ALU.mult).then_inc(newton_done, 1)
                elif n == 3:
                    dve.wait_ge(newton_done, g * 4 + 3)
                    nc.vector.scalar_tensor_tensor(out=rstd[:, s, :], in0=newton, scalar=1.5, in1=rs0, op0=ALU.add,
                                                   op1=ALU.mult).then_inc(newton_done, 1)
                else:
                    dve.wait_ge(newton_done, g * 4 + 4)
                    nc.vector.scalar_tensor_tensor(out=shift[:, s, :], in0=mean_sum[:, s % 2, :], scalar=-0.5,
                                                   in1=rstd[:, s, :], op0=ALU.mult, op1=ALU.mult)\
                        .then_inc(norm_ready, 1)

            def scales(g, s):
                for n in range(5):
                    scale_step(g, s, n)

            def take_h(g, s, pair, stored=None, last=False):
                if stored is not None:
                    dve.wait_ge(xh_stored[s], stored)
                banks = slice(4 + 2 * pair, 6 + 2 * pair)
                dve.wait_ge(h_ready, g * PG + pair + 1)
                nc.vector.tensor_copy(s_cols[:, bass.ts(g * PG + pair, 2), :], psum[:, banks, F:FD])\
                    .then_inc(s_ready, 1)
                if last:
                    dve.wait_ge(s_ready, NG * PG)
                    nc.vector.tensor_reduce(s2_max[:, 0:1], s2, AX_X, ALU.max).then_inc(s2_max_ready, 1)
                nc.vector.tensor_tensor(xh[s][:, 2 * pair:2 * pair + 2, :], psum[:, banks, 0:F],
                                        x_sb[:, bass.ts(g * PG + pair, 2), :], ALU.add).then_inc(h_used, 1)

            statistics_and_variance(0, 0)
            scales(0, 0)
            dve.wait_ge(weights_loaded, 32)
            for k in range(KF):
                for s in range(2):
                    nc.vector.tensor_tensor_reduce(out=products[:, 2 * k + s, :], in0=wx[:, k, 0:F],
                                                   in1=a_row[:, s, :], scale=1.0, scalar=0.0, op0=ALU.mult, op1=ALU.add,
                                                   accum_out=wx[:, k, F + s:F + s + 1]).then_inc(wx_ready, 1)
            statistics_and_variance(1, 1)
            scales(1, 1)
            statistics_and_variance(2, 2)
            statistics_and_variance(3, 3)
            scales(2, 2)

            def group(g, s, stored=None, loaded=None, ahead=4):
                take_h(g, s, 0, stored)
                if ahead >= 4:
                    dve.wait_ge(x_loaded[s], loaded)
                    for k in range(G):
                        last = statistics(g + 4, k)
                        if k == G - 1:
                            last.then_inc(stats_done, 1)
                        scale_step(g + 3, (s + 3) % XS, k)
                    scale_step(g + 3, (s + 3) % XS, G)
                    variance(g + 4, s)
                elif ahead == 3:
                    scales(g + 3, (s + 3) % XS)
                take_h(g, s, 1, last=(ahead == 0))

            for s in range(XS):
                group(s, s, loaded=32)
            with dve.Fori(1, NI - 1) as i:
                for s in range(XS):
                    group(i * XS + s, s, 32 * i, 16 * (i + 2))
            for s in range(XS):
                group((NI - 1) * XS + s, s, 32 * (NI - 1), ahead=XS - 1 - s)
            dve.wait_ge(c_ready, 1)
            nc.vector.tensor_scalar(tmp[:, 1, :], s1, s2_max[:, 1:2], 0.0, ALU.add, ALU.max)\
                .then_inc(arguments_ready, 1)
            nc.vector.tensor_scalar(tmp[:, 0, :], s2, s2_max[:, 1:2], None, ALU.subtract).then_inc(arguments_ready, 1)
            dve.wait_ge(r_ready, 1)
            nc.vector.tensor_copy(r_turned, psum[0:T, 0, 0:P]).then_inc(acc_free, TB // 2)
            dve.wait_ge(exps_ready, 3)
            nc.vector.tensor_scalar(neg_f1[:, :], f1[:, :], -0.5, None, ALU.mult).then_inc(factors_ready, 1)
            nc.vector.tensor_scalar(f2[:, :], f2[:, :], 0.5, None, ALU.mult).then_inc(factors_ready, 1)
            nc.vector.tensor_scalar(f1[:, :], f1[:, :], 0.5, None, ALU.mult).then_inc(factors_ready, 1)
            dve.wait_ge(factors_ready, 3)

            def first_masked():
                for half in range(2):
                    columns = slice(half * IB // 2, (half + 1) * IB // 2)
                    dve.wait_ge(first_w_ready if half == 0 else w_ready, 1)
                    if half == 0:
                        dve.wait_ge(adj_loaded[0], 16)
                    nc.vector.scalar_tensor_tensor(out=ring_f[:, 0, columns], in0=w_buf[:, 0, columns],
                                                   scalar=f1[:, 0:1], in1=ring[:, 0, columns], op0=ALU.add,
                                                   op1=ALU.min).then_inc(first_t_ready if half == 0 else t_ready, 1)
                    nc.vector.tensor_copy(r_buf[:, 0, columns], psum[:, TB // 2 + half, :])\
                        .then_inc(acc_free, 1 if half == 0 else TB // 2 - 1)

            def masked(step, jt, k, loaded):
                dve.wait_ge(w_ready, step + 1)
                if k % 2 == 0:
                    dve.wait_ge(adj_loaded[k // 2], loaded)
                nc.vector.scalar_tensor_tensor(out=ring_f[:, k, :], in0=w_buf[:, k % LS, :],
                                               scalar=f1[:, bass.ts(jt, 1)], in1=ring[:, k, :], op0=ALU.add,
                                               op1=ALU.min).then_inc(t_ready, 1)

            def low(step, k, free=True):
                dve.wait_ge(p_hi_ready, step + 1)
                if free:
                    dve.wait_ge(step_done, step - (LS - 1))
                nc.vector.scalar_tensor_tensor(out=p_lo[:, k % LS, :], in0=ring_f[:, k, :], scalar=0.0,
                                               in1=p_hi[:, k % HS, :].bitcast(F32), op0=ALU.max, op1=ALU.subtract)\
                    .then_inc(p_lo_ready, 1)

            def denominators(b):
                dve.wait_ge(acc_free, (b + 2) * TB)
                nc.vector.tensor_tensor(lowest[:, :], lowest[:, :], acc[:, :, F], ALU.min)
                nc.vector.tensor_scalar(denom[:, 0, :], acc[:, :, F], TINY, None, ALU.max).then_inc(denom_done, 1)
                dve.wait_ge(denom_done, 2 * b + 1)
                nc.vector.reciprocal(denom[:, 1, :], denom[:, 0, :]).then_inc(denom_done, 1)
                dve.wait_ge(denom_done, 2 * b + 2)

            def scale(k):
                for it in (2 * k, 2 * k + 1):
                    nc.vector.tensor_scalar(acc[:, it, 0:F], acc[:, it, 0:F], denom[:, 1, it:it + 1], None,
                                            ALU.mult).then_inc(scaled, 1)

            def block_of_rows(b, first):
                if first:
                    first_masked()
                else:
                    masked(b * T, 0, 0, 16 * (b * Q + 1))
                for k in range(U):
                    turn = b * Q + (2 if k == U - 1 else 1)
                    masked(b * T + k + 1, k + 1, (k + 1) % U, 16 * turn)
                    low(b * T + k, k, not first or k >= LS)
                    if k == 3 and not first:
                        denominators(b - 1)
                    if k >= U - TB // 2 and not first:
                        scale(k - (U - TB // 2))
                with dve.Fori(1, Q - 1) as q:
                    for k in range(U):
                        turn = b * Q + q + (2 if k == U - 1 else 1)
                        masked(b * T + q * U + k + 1, q * U + k + 1, (k + 1) % U, 16 * turn)
                        low(b * T + q * U + k, k)
                for k in range(U):
                    if k < U - 1:
                        masked(b * T + (T - U) + k + 1, T - U + k + 1, k + 1, 16 * (b * Q + Q))
                    low(b * T + (T - U) + k, k)

            block_of_rows(0, True)
            with dve.Fori(1, NB) as b:
                block_of_rows(b, False)
            dve.wait_ge(acc_stored, 16 * NB)
            for half in range(2):
                banks = slice(half * TB // 2, (half + 1) * TB // 2)
                if half == 0:
                    dve.wait_ge(acc_ready, (NB - 1) * (TB - 1) + TB // 2)
                else:
                    dve.wait_ge(step_done, NB * T)
                done = 2 * (NB - 1 + half)
                nc.vector.tensor_scalar(denom[:, 0, banks], psum[:, banks, F], TINY, None, ALU.max)\
                    .then_inc(denom_done, 1)
                dve.wait_ge(denom_done, done + 1)
                nc.vector.reciprocal(denom[:, 1, banks], denom[:, 0, banks]).then_inc(denom_done, 1)
                dve.wait_ge(denom_done, done + 2)
                for it in (banks.start, banks.start + 2):
                    last = nc.vector.tensor_scalar(acc[:, it, 0:F], psum[:, it, 0:F], denom[:, 1, it:it + 1], None,
                                                   ALU.mult)
                last.then_inc(scaled, 1)
            nc.vector.tensor_tensor(lowest[:, :], lowest[:, :], denom[:, 0, :], ALU.min).then_inc(lowest_done, 1)
            dve.wait_ge(lowest_done, 1)

            nc.vector.tensor_reduce(too_low[:, 0:1], lowest[:, :], AX_X, ALU.min).then_inc(lowest_done, 1)
            dve.wait_ge(lowest_done, 2)
            nc.vector.tensor_scalar(too_low[:, 0:1], too_low[:, 0:1], LOWEST_SUM, None, ALU.is_lt)\
                .then_inc(lowest_done, 1)
            dve.wait_ge(too_low_ready, 1)
            nc.vector.tensor_copy(second_pass[:, :], too_low[:, 1:2]).then_inc(second_pass_ready, 1)

            dve.wait_ge(second_pass_ready, 1)
            with dve.If(dve.value_load(second_pass[0:1, 0:1]) > 0):
                nc.vector.memset(ones_square.bitcast(F32), 1.0).then_inc(ones_square_ready, 1)
                nc.vector.memset(work, 0.0).then_inc(pair_used, 1)
                with dve.Fori(0, NB) as b:
                    nc.vector.memset(row_max, NO_EDGE).then_inc(candidates_done, 1)
                    with dve.Fori(0, NP) as n:
                        dve.wait_ge(pair_loaded, 16 * (2 * b * NP + n + 1))
                        for k in range(2):
                            done = b * (3 * T + 1) + 1 + 3 * (2 * n + k)
                            dve.wait_ge(candidates_done, done)
                            nc.vector.tensor_scalar(gate, ring[:, k, :], 0.0, -2.0 * NO_EDGE, ALU.is_gt, ALU.mult)\
                                .then_inc(candidates_done, 1)
                            dve.wait_ge(candidates_done, done + 1)
                            nc.vector.tensor_scalar(work, gate, NO_EDGE, s2[:, bass.ds(2 * n + k, 1)], ALU.add,
                                                    ALU.min).then_inc(candidates_done, 1)
                            dve.wait_ge(candidates_done, done + 2)
                            last = nc.vector.tensor_tensor(row_max, row_max, work, ALU.max)
                            last.then_inc(candidates_done, 1)
                        dve.wait_ge(candidates_done, done + 3)
                        nc.vector.memset(gate, 0.0).then_inc(pair_used, 1)
                    dve.wait_ge(row_max_ready, b + 1)
                    dve.wait_ge(s1_row_loaded, 16 * (b + 1))
                    nc.vector.tensor_tensor(work, s1_row, work2, ALU.add).then_inc(top_done, 1)
                    dve.wait_ge(top_done, 2 * b + 1)
                    nc.vector.scalar_tensor_tensor(out=top_row, in0=work, scalar=SLOPE, in1=work, op0=ALU.mult,
                                                   op1=ALU.max).then_inc(top_done, 1)
                    with dve.Fori(0, NP) as n:
                        dve.wait_ge(top_done, 2 * b + 2)
                        dve.wait_ge(pair_loaded, 16 * ((2 * b + 1) * NP + n + 1))
                        for k in range(2):
                            tile = b * T + 2 * n + k
                            nc.vector.tensor_scalar(work, s1_row, s2[:, bass.ds(2 * n + k, 1)], None, ALU.add)\
                                .then_inc(logits_done, 1)
                            dve.wait_ge(logits_done, 4 * tile + 1)
                            nc.vector.scalar_tensor_tensor(out=work2, in0=work, scalar=SLOPE, in1=work,
                                                           op0=ALU.mult, op1=ALU.max).then_inc(logits_done, 1)
                            dve.wait_ge(logits_done, 4 * tile + 2)
                            nc.vector.tensor_tensor(work, work2, top_row, ALU.subtract).then_inc(logits_done, 1)
                            dve.wait_ge(logits_done, 4 * tile + 3)
                            nc.vector.tensor_scalar(work2, work, 1.0, None, ALU.min).then_inc(logits_done, 1)
                            dve.wait_ge(exps_done, tile + 1)
                            nc.vector.scalar_tensor_tensor(out=weights2, in0=ring[:, k, :], scalar=0.0, in1=exps,
                                                           op0=ALU.is_gt, op1=ALU.mult).then_inc(weights_done, 1)
                            dve.wait_ge(weights_hi_ready, tile + 1)
                            nc.vector.tensor_tensor(p_lo[:, 0, :], weights2, p_hi[:, 0, :].bitcast(F32),
                                                    ALU.subtract).then_inc(weights_lo_ready, 1)
                        dve.wait_ge(weights_lo_ready, b * T + 2 * n + 2)
                        nc.vector.memset(gate, 0.0).then_inc(pair_used, 1)
                    no_edge = denom[:, 0, :]
                    dve.wait_ge(banks_taken, (b + 1) * TB + 1)
                    nc.vector.tensor_scalar(no_edge, acc[:, :, F], 0.0, None, ALU.is_equal).then_inc(mean_done, 1)
                    dve.wait_ge(mean_done, 3 * b + 1)
                    nc.vector.scalar_tensor_tensor(out=denom[:, 1, :], in0=no_edge, scalar=float(N),
                                                   in1=acc[:, :, F], op0=ALU.mult, op1=ALU.add)
                    for it in range(TB):
                        last = nc.vector.scalar_tensor_tensor(out=acc[:, it, 0:F], in0=node_sums,
                                                              scalar=no_edge[:, it:it + 1], in1=acc[:, it, 0:F],
                                                              op0=ALU.mult, op1=ALU.add)
                    last.then_inc(mean_done, 1)
                    dve.wait_ge(mean_done, 3 * b + 2)
                    nc.vector.reciprocal(denom[:, 1, :], denom[:, 1, :]).then_inc(mean_done, 1)
                    dve.wait_ge(mean_done, 3 * b + 3)
                    dve.wait_ge(xh_rows_loaded, 16 * (b + 1))
                    for it in range(TB):
                        last = nc.vector.scalar_tensor_tensor(out=acc[:, it, 0:F], in0=acc[:, it, 0:F],
                                                              scalar=denom[:, 1, it:it + 1], in1=xh_rows[:, it, :],
                                                              op0=ALU.mult, op1=ALU.add)
                    last.then_inc(rows_ready, 1)

        @block.tensor
        def _(pe):
            pe.wait_ge(ident_ready, 2)
            pe.wait_ge(wx_ready, KF * 2)

            def turn_pair(g, s, pair):
                pe.wait_ge(node_ready, g * G + 2 * pair + 2)
                for n in range(2 * KF):
                    k, kf = 2 * pair + n // KF, n % KF
                    last = nc.tensor.transpose(psum[:, pair, n * P:(n + 1) * P], node[s][:, k, kf * P:(kf + 1) * P],
                                               ident[:, :])
                last.then_inc(turned, 1)

            def product(g, pair):
                pe.wait_ge(node_t_ready, g * PG + pair + 1)
                pe.wait_ge(h_used, g * PG + pair + 1)
                for n in range(2 * KF):
                    k, kf = n // KF, n % KF
                    last = nc.tensor.matmul(psum[:, 4 + 2 * pair + k, 0:FD], node_t[pair][:, n * P:(n + 1) * P],
                                            wx[:, kf, :], start=(kf == 0), stop=(kf == KF - 1))
                last.then_inc(h_ready, 1)

            turn_pair(0, 0, 0)
            with pe.Fori(0, NI - 1) as i:
                for s in range(XS):
                    turn_pair(i * XS + s, s, 1)
                    product(i * XS + s, 0)
                    turn_pair(i * XS + s + 1, (s + 1) % XS, 0)
                    product(i * XS + s, 1)
            for s in range(XS):
                g = (NI - 1) * XS + s
                turn_pair(g, s, 1)
                product(g, 0)
                if s + 1 < XS:
                    turn_pair(g + 1, s + 1, 0)
                product(g, 1)
            pe.wait_ge(exps_ready, 1)
            nc.tensor.transpose(psum[0:T, 0, 0:P], r_cols, ident[:, :]).then_inc(r_ready, 1)
            pe.wait_ge(acc_free, TB // 2)
            for it in range(TB):
                last = nc.tensor.matmul(psum[:, TB // 2 + it // 4, (it % 4) * P:(it % 4 + 1) * P],
                                        ident[0:T, it:it + 1].to_broadcast([T, P]), r_turned, start=True, stop=True)
                if it % 4 == 3:
                    last.then_inc(r_ready, 1)
            pe.wait_ge(ones_ready, 1)
            pe.wait_ge(lo_ready, NG)

            def step(b, n, jt, k, first=False, last=False):
                hi, lo = (v[:, bass.ts(jt, 1), :].rearrange("p o f -> p (o f)") for v in (node_hi, node_lo))

                def high_products(it):
                    if first:
                        pe.wait_ge(acc_free, b * TB + it + 1)
                    p = p_hi[:, k % HS, it * P:(it + 1) * P]
                    nc.tensor.matmul(psum[:, it, 0:FD], p, hi, start=first, stop=False)
                    nc.tensor.matmul(psum[:, it, 0:F], p, lo, start=False, stop=False)

                def low_product(it):
                    return nc.tensor.matmul(psum[:, it, 0:FD], p_lo[:, k % LS, it * P:(it + 1) * P], hi, start=False,
                                            stop=last)

                if first:
                    pe.wait_ge(half_hi_ready, b + 1)
                else:
                    pe.wait_ge(p_hi_ready, n + 1)
                if last:
                    pe.wait_ge(p_lo_ready, n + 1)
                    for it in range(TB):
                        high_products(it)
                        low_product(it).then_inc(acc_ready if it < TB - 1 else step_done, 1)
                    return
                for it in range(TB):
                    if first and it == TB // 2:
                        pe.wait_ge(p_hi_ready, n + 1)
                    high_products(it)
                pe.wait_ge(p_lo_ready, n + 1)
                for it in range(TB):
                    mm = low_product(it)
                mm.then_inc(step_done, 1)

            with pe.Fori(0, NB) as b:
                for k in range(U):
                    step(b, b * T + k, k, k, first=(k == 0))
                with pe.Fori(1, Q - 1) as q:
                    for k in range(U):
                        step(b, b * T + q * U + k, q * U + k, k)
                for k in range(U):
                    step(b, b * T + (T - U) + k, T - U + k, k, last=(k == U - 1))

            pe.wait_ge(second_pass_ready, 1)
            with pe.If(pe.value_load(second_pass[0:1, 0:1]) > 0):
                def parts(jt):
                    return (v[:, bass.ds(jt, 1), :].rearrange("p o f -> p (o f)") for v in (node_hi, node_lo))

                def node_sum(jt, first=False, last=False):
                    hi, lo = parts(jt)
                    nc.tensor.matmul(psum[:, 0, 0:F], ones_square, hi[:, 0:F], start=first, stop=False)
                    return nc.tensor.matmul(psum[:, 0, 0:F], ones_square, lo, start=False, stop=last)

                def tile(b, jt, first=False, last=False):
                    hi, lo = parts(jt)
                    if first:
                        pe.wait_ge(banks_taken, b * TB + 1)
                    pe.wait_ge(weights_lo_ready, b * T + jt + 1)
                    for it in range(TB):
                        columns = slice(it * P, (it + 1) * P)
                        nc.tensor.matmul(psum[:, it, 0:FD], p_hi[:, 0, columns], hi, start=first, stop=False)
                        nc.tensor.matmul(psum[:, it, 0:F], p_hi[:, 0, columns], lo, start=False, stop=False)
                        mm = nc.tensor.matmul(psum[:, it, 0:FD], p_lo[:, 0, columns], hi, start=False, stop=last)
                    mm.then_inc(tile_done, 1)

                pe.wait_ge(ones_square_ready, 1)
                node_sum(0, first=True)
                with pe.Fori(1, T - 1) as jt:
                    node_sum(jt)
                node_sum(T - 1, last=True).then_inc(tile_done, 1)
                with pe.Fori(0, NB) as b:
                    tile(b, 0, first=True)
                    with pe.Fori(1, T - 1) as jt:
                        tile(b, jt)
                    tile(b, T - 1, last=True)


def kernel(x, adj, L0_gnn_W, L0_gnn_a):
    import numpy as np
    import concourse.bacc as bacc
    from concourse.bass_utils import run_bass_kernel_spmd

    nodes, feats = x.shape
    block_rows = 1024
    nb, t = nodes // block_rows, nodes // P
    arrays = {
        "x": np.ascontiguousarray(x),
        "adj_t": np.ascontiguousarray(np.asarray(adj).reshape(nb, block_rows, t, P).transpose(0, 2, 3, 1)),
        "w": np.ascontiguousarray(L0_gnn_W),
        "a": np.ascontiguousarray(L0_gnn_a),
    }
    nc = bacc.Bacc("TRN2", target_bir_lowering=False, num_devices=1, dynamic_dma_scratch_size=8192)
    args = [nc.dram_tensor(name, v.shape, mybir.dt.from_np(v.dtype), kind="ExternalInput").ap()
            for name, v in arrays.items()]
    out = nc.dram_tensor("out", (nodes, feats), F32, kind="ExternalOutput").ap()
    gat_layer(nc, *args, out)
    r = run_bass_kernel_spmd(nc, [arrays], core_ids=[0])
    return r.results[0]["out"]
```
